# Optimizing a Trainium2 kernel written in Bass

```python
import numpy as np
import jax
import jax.numpy as jnp

def _softmax(x, axis=-1):
    return jax.nn.softmax(x, axis=axis)

def _gelu(x):
    return jax.nn.gelu(x, approximate=True)

def _silu(x):
    return jax.nn.silu(x)

def _sigmoid(x):
    return jax.nn.sigmoid(x)

def _layernorm(x, axis=-1, eps=1e-05):
    m = jnp.mean(x, axis=axis, keepdims=True)
    v = jnp.var(x, axis=axis, keepdims=True)
    return (x - m) / jnp.sqrt(v + eps)

def _scatter_add(tgt, idx, src, axis=0):
    return tgt.at[idx].add(src)

def _segment_sum(src, seg, n):
    return jax.ops.segment_sum(src, seg, n)
kernel_name = 'mk_xattn_ffn_d4_seqx_r8_d3969a'

def setup_inputs(seed: int=0):
    np.random.seed(seed)
    _w = jnp.asarray

    def _rec_inputs():
        import jax
        import jax.numpy as jnp
        _rk = jax.random.key(seed)
        x = -0.000125 + 0.9999 * jax.random.normal(jax.random.fold_in(_rk, 1), (2, 256, 512), jnp.float32)
        _lenS = 256 - jax.random.randint(jax.random.fold_in(_rk, 7), (2,), 0, max(1, 256 // 4) + 1, jnp.int32)
        _lenS2 = 512 - jax.random.randint(jax.random.fold_in(_rk, 8), (2,), 0, max(1, 512 // 4) + 1, jnp.int32)
        _ctx_4096P = jax.random.normal(jax.random.fold_in(_rk, 11), (2, 16, 512), jnp.float32)
        _ctx_4096c = jax.random.dirichlet(jax.random.fold_in(_rk, 511), 0.3 * jnp.ones((16,), jnp.float32), (2, 512))
        _ctx_4096t = jnp.einsum('bsk,bkd->bsd', _ctx_4096c, _ctx_4096P)
        _ctx_4096t = _ctx_4096t * jax.lax.rsqrt(jnp.mean(jnp.square(_ctx_4096t)) + 1e-12) * 0.953939
        ctx_4096 = -5.72187e-05 + 0.999849 * (_ctx_4096t + 0.3 * jax.random.normal(jax.random.fold_in(_rk, 611), (2, 512, 512), jnp.float32))
        return (x, ctx_4096)
    x, ctx_4096 = _rec_inputs()

    def _L0_xattn_setup():
        import jax, jax.numpy as jnp
        import numpy as np
        QMIN = 0.0
        QMAX = 255.0

        def fake_quant(x, scale, zp):
            s = scale.reshape(())
            z = zp.reshape(())
            q = jnp.clip(jnp.round(x / s + z), QMIN, QMAX)
            return (q - z) * s
        key = jax.random.key(seed)
        k1, k2 = jax.random.split(key)
        B, M, K, N = (4, 256, 512, 512)
        x1 = jax.random.normal(k1, (B, M, K), dtype=jnp.float32)
        x2 = jax.random.normal(k2, (B, K, N), dtype=jnp.float32)
        x1_scale = jnp.full((1,), 8.0 / 255.0, dtype=jnp.float32)
        x1_zp = jnp.full((1,), 128.0, dtype=jnp.float32)
        x2_scale = jnp.full((1,), 8.0 / 255.0, dtype=jnp.float32)
        x2_zp = jnp.full((1,), 128.0, dtype=jnp.float32)
        return {'x1': x1, 'x2': x2, 'x1_scale': x1_scale, 'x1_zp': x1_zp, 'x2_scale': x2_scale, 'x2_zp': x2_zp}
    _L0_xattn_all = _L0_xattn_setup()
    _L0_xattn_in = {k: v for k, v in _L0_xattn_all.items() if k in ('x1_scale', 'x1_zp', 'x2_scale', 'x2_zp')}
    del _L0_xattn_all

    def _L0_ffn_setup():
        import jax, jax.numpy as jnp
        import numpy as np
        HIDDEN = 512
        INTER = 1376
        BATCH, SEQ = (2, 256)

        def _ternary(key, shape):
            return jax.random.randint(key, shape, -1, 2).astype(jnp.float32)
        key = jax.random.key(seed)
        kx, kg, ku, kd = jax.random.split(key, 4)
        x = jax.random.normal(kx, (BATCH, SEQ, HIDDEN), dtype=jnp.float32)
        gate_w = _ternary(kg, (INTER, HIDDEN))
        up_w = _ternary(ku, (INTER, HIDDEN))
        down_w = _ternary(kd, (HIDDEN, INTER))
        gate_scale = jnp.float32(0.02)
        up_scale = jnp.float32(0.02)
        down_scale = jnp.float32(0.02)
        return {'x': x, 'gate_w': gate_w, 'up_w': up_w, 'down_w': down_w, 'gate_scale': gate_scale, 'up_scale': up_scale, 'down_scale': down_scale}
    _L0_ffn_all = _L0_ffn_setup()
    _L0_ffn_in = {k: v for k, v in _L0_ffn_all.items() if k in ('gate_w', 'up_w', 'down_w', 'gate_scale', 'up_scale', 'down_scale')}
    del _L0_ffn_all

    def _L1_xattn_setup():
        import jax, jax.numpy as jnp
        import numpy as np
        import math
        HIDDEN = 512
        N_HEADS = 32
        HEAD_DIM = 128
        N_KV_HEADS = 4
        N_GROUPS = N_HEADS // N_KV_HEADS
        key = jax.random.key(seed)
        ks = jax.random.split(key, 6)
        B, NL, S = (8, 64, 512)
        latents = jax.random.normal(ks[0], (B, NL, HIDDEN), dtype=jnp.float32)
        context = jax.random.normal(ks[1], (B, S, HIDDEN), dtype=jnp.float32)
        scale = 1.0 / math.sqrt(HIDDEN)
        Wq = jax.random.normal(ks[2], (HIDDEN, N_HEADS * HEAD_DIM), dtype=jnp.float32) * scale
        Wk = jax.random.normal(ks[3], (HIDDEN, N_KV_HEADS * HEAD_DIM), dtype=jnp.float32) * scale
        Wv = jax.random.normal(ks[4], (HIDDEN, N_KV_HEADS * HEAD_DIM), dtype=jnp.float32) * scale
        Wo = jax.random.normal(ks[5], (N_HEADS * HEAD_DIM, HIDDEN), dtype=jnp.float32) * scale
        return {'latents': latents, 'context': context, 'Wq': Wq, 'Wk': Wk, 'Wv': Wv, 'Wo': Wo}
    _L1_xattn_all = _L1_xattn_setup()
    _L1_xattn_in = {k: v for k, v in _L1_xattn_all.items() if k in ('Wq', 'Wk', 'Wv', 'Wo')}
    del _L1_xattn_all

    def _L1_ffn_setup():
        import jax, jax.numpy as jnp
        import numpy as np
        TOP_K = 2
        key = jax.random.key(seed)
        k1, k2, k3 = jax.random.split(key, 3)
        B, S, H, O, E = (1024, 1, 512, 512, 8)
        x = jax.random.normal(k1, (B, S, H), dtype=jnp.float32)
        gate_w = jax.random.normal(k2, (H, E), dtype=jnp.float32) * 0.02
        expert_w = jax.random.normal(k3, (E, H, O), dtype=jnp.float32) * 0.02
        return {'x': x, 'gate_w': gate_w, 'expert_w': expert_w}
    _L1_ffn_all = _L1_ffn_setup()
    _L1_ffn_in = {k: v for k, v in _L1_ffn_all.items() if k in ('gate_w', 'expert_w')}
    del _L1_ffn_all

    def _L2_xattn_setup():
        import jax, jax.numpy as jnp
        import numpy as np
        HEADS = 32
        KV_HEADS = 8
        HEAD_DIM = 128
        EPS = 1e-06

        def rms_norm(x, w):
            var = jnp.mean(jnp.square(x.astype(jnp.float32)), axis=-1, keepdims=True)
            return (x.astype(jnp.float32) * jax.lax.rsqrt(var + EPS)).astype(x.dtype) * w
        key = jax.random.key(seed)
        ks = jax.random.split(key, 6)
        bsz, n_lat, seq, hidden = (8, 64, 512, 512)
        return {'latents': jax.random.normal(ks[0], (bsz, n_lat, hidden), jnp.float32), 'context': jax.random.normal(ks[1], (bsz, seq, hidden), jnp.float32), 'Wq': jax.random.normal(ks[2], (hidden, HEADS * HEAD_DIM), jnp.float32) * 0.02, 'Wk': jax.random.normal(ks[3], (hidden, KV_HEADS * HEAD_DIM), jnp.float32) * 0.02, 'Wv': jax.random.normal(ks[4], (hidden, KV_HEADS * HEAD_DIM), jnp.float32) * 0.02, 'Wo': jax.random.normal(ks[5], (HEADS * HEAD_DIM, hidden), jnp.float32) * 0.02, 'q_norm_w': jnp.ones((HEAD_DIM,), jnp.float32), 'k_norm_w': jnp.ones((HEAD_DIM,), jnp.float32)}
    _L2_xattn_all = _L2_xattn_setup()
    _L2_xattn_in = {k: v for k, v in _L2_xattn_all.items() if k in ('Wq', 'Wk', 'Wv', 'Wo', 'q_norm_w', 'k_norm_w')}
    del _L2_xattn_all

    def _L2_ffn_setup():
        import jax, jax.numpy as jnp
        import numpy as np
        GROUP = 64

        def dequant_q40(w, s, out_features, in_features):
            msb = w >> 4
            lsb = (w & 15 ^ 8) - 8
            g = jnp.concatenate([msb, lsb], axis=1).reshape(-1, GROUP)
            deq = g.astype(s.dtype) * s[:, None]
            return deq.reshape(out_features, in_features)
        key = jax.random.key(seed)
        ks = jax.random.split(key, 7)
        dim, hidden = (512, 1376)
        B, S = (2, 256)

        def packed(k, din, dout):
            return jax.random.randint(k, (din * dout // GROUP // 2, GROUP), -128, 128, dtype=jnp.int32)

        def scales(k, din, dout):
            return (jax.random.uniform(k, (din * dout // GROUP,), dtype=jnp.float32) + 0.5) * 0.01
        x = jax.random.normal(ks[0], (B, S, dim), dtype=jnp.float32)
        w1 = packed(ks[1], dim, hidden)
        s1 = scales(ks[2], dim, hidden)
        w2 = packed(ks[3], hidden, dim)
        s2 = scales(ks[4], hidden, dim)
        w3 = packed(ks[5], dim, hidden)
        s3 = scales(ks[6], dim, hidden)
        return {'x': x, 'w1': w1, 's1': s1, 'w2': w2, 's2': s2, 'w3': w3, 's3': s3}
    _L2_ffn_all = _L2_ffn_setup()
    _L2_ffn_in = {k: v for k, v in _L2_ffn_all.items() if k in ('w1', 's1', 'w2', 's2', 'w3', 's3')}
    del _L2_ffn_all

    def _L3_xattn_setup():
        import jax, jax.numpy as jnp
        import numpy as np
        TEXT_DIM = 512
        FEATURE_DIM = 512

        def _xavier_uniform(key, shape):
            fan_in, fan_out = (shape[1], shape[0])
            limit = float(np.sqrt(6.0 / (fan_in + fan_out)))
            return jax.random.uniform(key, shape, jnp.float32, -limit, limit)
        key = jax.random.key(seed)
        k1, k2, k3, k4 = jax.random.split(key, 4)
        text = jax.random.normal(k1, (8, 256, TEXT_DIM), jnp.float32)
        features = jax.random.normal(k2, (8, 72, FEATURE_DIM), jnp.float32)
        Wq = _xavier_uniform(k3, (FEATURE_DIM, TEXT_DIM))
        bq = jnp.zeros((FEATURE_DIM,), jnp.float32)
        Wk = _xavier_uniform(k4, (FEATURE_DIM, FEATURE_DIM))
        bk = jnp.zeros((FEATURE_DIM,), jnp.float32)
        return {'text': text, 'features': features, 'Wq': Wq, 'bq': bq, 'Wk': Wk, 'bk': bk}
    _L3_xattn_all = _L3_xattn_setup()
    _L3_xattn_in = {k: v for k, v in _L3_xattn_all.items() if k in ('Wq', 'bq', 'Wk', 'bk')}
    del _L3_xattn_all

    def _L3_ffn_setup():
        import jax, jax.numpy as jnp
        import numpy as np
        K_TOP = 8
        key = jax.random.key(seed)
        k1, k2, k3 = jax.random.split(key, 3)
        B, S, H, E = (4, 512, 512, 64)
        hidden_states = jax.random.normal(k1, (B, S, H), dtype=jnp.float32)
        router_weight = jax.random.normal(k2, (E, H), dtype=jnp.float32)
        router_bias = jnp.zeros((E,), dtype=jnp.float32)
        expert_bias = jax.random.normal(k3, (E, H), dtype=jnp.float32) * 0.1
        return {'hidden_states': hidden_states, 'router_weight': router_weight, 'router_bias': router_bias, 'expert_bias': expert_bias}
    _L3_ffn_all = _L3_ffn_setup()
    _L3_ffn_in = {k: v for k, v in _L3_ffn_all.items() if k in ('router_weight', 'router_bias', 'expert_bias')}
    del _L3_ffn_all
    return {'x': x, 'ctx_4096': ctx_4096, 'L0_xattn_x1_scale': _L0_xattn_in['x1_scale'], 'L0_xattn_x1_zp': _L0_xattn_in['x1_zp'], 'L0_xattn_x2_scale': _L0_xattn_in['x2_scale'], 'L0_xattn_x2_zp': _L0_xattn_in['x2_zp'], 'L0_ffn_gate_w': _L0_ffn_in['gate_w'], 'L0_ffn_up_w': _L0_ffn_in['up_w'], 'L0_ffn_down_w': _L0_ffn_in['down_w'], 'L0_ffn_gate_scale': _L0_ffn_in['gate_scale'], 'L0_ffn_up_scale': _L0_ffn_in['up_scale'], 'L0_ffn_down_scale': _L0_ffn_in['down_scale'], 'L1_xattn_Wq': _L1_xattn_in['Wq'], 'L1_xattn_Wk': _L1_xattn_in['Wk'], 'L1_xattn_Wv': _L1_xattn_in['Wv'], 'L1_xattn_Wo': _L1_xattn_in['Wo'], 'L1_ffn_gate_w': _L1_ffn_in['gate_w'], 'L1_ffn_expert_w': _L1_ffn_in['expert_w'], 'L2_xattn_Wq': _L2_xattn_in['Wq'], 'L2_xattn_Wk': _L2_xattn_in['Wk'], 'L2_xattn_Wv': _L2_xattn_in['Wv'], 'L2_xattn_Wo': _L2_xattn_in['Wo'], 'L2_xattn_q_norm_w': _L2_xattn_in['q_norm_w'], 'L2_xattn_k_norm_w': _L2_xattn_in['k_norm_w'], 'L2_ffn_w1': _L2_ffn_in['w1'], 'L2_ffn_s1': _L2_ffn_in['s1'], 'L2_ffn_w2': _L2_ffn_in['w2'], 'L2_ffn_s2': _L2_ffn_in['s2'], 'L2_ffn_w3': _L2_ffn_in['w3'], 'L2_ffn_s3': _L2_ffn_in['s3'], 'L3_xattn_Wq': _L3_xattn_in['Wq'], 'L3_xattn_bq': _L3_xattn_in['bq'], 'L3_xattn_Wk': _L3_xattn_in['Wk'], 'L3_xattn_bk': _L3_xattn_in['bk'], 'L3_ffn_router_weight': _L3_ffn_in['router_weight'], 'L3_ffn_router_bias': _L3_ffn_in['router_bias'], 'L3_ffn_expert_bias': _L3_ffn_in['expert_bias']}

def reference(x, ctx_4096, L0_xattn_x1_scale, L0_xattn_x1_zp, L0_xattn_x2_scale, L0_xattn_x2_zp, L0_ffn_gate_w, L0_ffn_up_w, L0_ffn_down_w, L0_ffn_gate_scale, L0_ffn_up_scale, L0_ffn_down_scale, L1_xattn_Wq, L1_xattn_Wk, L1_xattn_Wv, L1_xattn_Wo, L1_ffn_gate_w, L1_ffn_expert_w, L2_xattn_Wq, L2_xattn_Wk, L2_xattn_Wv, L2_xattn_Wo, L2_xattn_q_norm_w, L2_xattn_k_norm_w, L2_ffn_w1, L2_ffn_s1, L2_ffn_w2, L2_ffn_s2, L2_ffn_w3, L2_ffn_s3, L3_xattn_Wq, L3_xattn_bq, L3_xattn_Wk, L3_xattn_bk, L3_ffn_router_weight, L3_ffn_router_bias, L3_ffn_expert_bias):
    import jax
    import jax.numpy as jnp

    def _L0_xattn_ref(x1, x2, x1_scale, x1_zp, x2_scale, x2_zp):
        import jax, jax.numpy as jnp
        import numpy as np
        QMIN = 0.0
        QMAX = 255.0

        def fake_quant(x, scale, zp):
            s = scale.reshape(())
            z = zp.reshape(())
            q = jnp.clip(jnp.round(x / s + z), QMIN, QMAX)
            return (q - z) * s
        q1 = fake_quant(x1, x1_scale, x1_zp)
        q2 = fake_quant(x2, x2_scale, x2_zp)
        return jnp.matmul(q1, q2)

    def _L0_ffn_ref(x, gate_w, up_w, down_w, gate_scale, up_scale, down_scale):
        import jax, jax.numpy as jnp
        import numpy as np
        HIDDEN = 512
        INTER = 1376
        BATCH, SEQ = (2, 256)

        def _ternary(key, shape):
            return jax.random.randint(key, shape, -1, 2).astype(jnp.float32)
        gate = jnp.einsum('bsh,ih->bsi', x, gate_w) * gate_scale
        up = jnp.einsum('bsh,ih->bsi', x, up_w) * up_scale
        inter = jax.nn.silu(gate) * up
        out = jnp.einsum('bsi,hi->bsh', inter, down_w) * down_scale
        return out

    def _L1_xattn_ref(latents, context, Wq, Wk, Wv, Wo):
        import jax, jax.numpy as jnp
        import numpy as np
        import math
        HIDDEN = 512
        N_HEADS = 32
        HEAD_DIM = 128
        N_KV_HEADS = 4
        N_GROUPS = N_HEADS // N_KV_HEADS
        b, q_len, _ = latents.shape
        kv_len = q_len + context.shape[1]
        hidden_states = jnp.concatenate([context, latents], axis=1)
        q = (latents @ Wq).reshape(b, q_len, N_KV_HEADS, N_GROUPS, HEAD_DIM)
        k = (hidden_states @ Wk).reshape(b, kv_len, N_KV_HEADS, HEAD_DIM)
        v = (hidden_states @ Wv).reshape(b, kv_len, N_KV_HEADS, HEAD_DIM)
        scale = 1.0 / math.sqrt(HEAD_DIM)
        scores = jnp.einsum('bqhgd,bkhd->bhgqk', q, k) * scale
        attn = jax.nn.softmax(scores.astype(jnp.float32), axis=-1).astype(q.dtype)
        out = jnp.einsum('bhgqk,bkhd->bqhgd', attn, v)
        out = out.reshape(b, q_len, N_HEADS * HEAD_DIM)
        return out @ Wo

    def _L1_ffn_ref(x, gate_w, expert_w):
        import jax, jax.numpy as jnp
        import numpy as np
        TOP_K = 2
        E = gate_w.shape[-1]
        logits = jnp.einsum('bsh,he->bse', x, gate_w)
        topv, topi = jax.lax.top_k(logits, TOP_K)
        w = jax.nn.softmax(topv, axis=-1)
        onehot = jax.nn.one_hot(topi, E, dtype=x.dtype)
        w_e = jnp.einsum('bske,bsk->bse', onehot, w)
        out = jnp.einsum('bsh,eho,bse->bso', x, expert_w, w_e)
        return out

    def _L2_xattn_ref(latents, context, Wq, Wk, Wv, Wo, q_norm_w, k_norm_w):
        import jax, jax.numpy as jnp
        import numpy as np
        HEADS = 32
        KV_HEADS = 8
        HEAD_DIM = 128
        EPS = 1e-06

        def rms_norm(x, w):
            var = jnp.mean(jnp.square(x.astype(jnp.float32)), axis=-1, keepdims=True)
            return (x.astype(jnp.float32) * jax.lax.rsqrt(var + EPS)).astype(x.dtype) * w
        bsz, q_len, hidden = latents.shape
        kv = jnp.concatenate([context, latents], axis=1)
        kv_len = kv.shape[1]
        groups = HEADS // KV_HEADS
        q = (latents @ Wq).reshape(bsz, q_len, HEADS, HEAD_DIM).transpose(0, 2, 1, 3)
        k = (kv @ Wk).reshape(bsz, kv_len, KV_HEADS, HEAD_DIM).transpose(0, 2, 1, 3)
        v = (kv @ Wv).reshape(bsz, kv_len, KV_HEADS, HEAD_DIM).transpose(0, 2, 1, 3)
        q = rms_norm(q, q_norm_w)
        k = rms_norm(k, k_norm_w)
        qg = q.reshape(bsz, KV_HEADS, groups, q_len, HEAD_DIM)
        scale = 1.0 / np.sqrt(HEAD_DIM)
        scores = jnp.einsum('bhgqd,bhkd->bhgqk', qg, k) * scale
        probs = jax.nn.softmax(scores.astype(jnp.float32), axis=-1).astype(q.dtype)
        out = jnp.einsum('bhgqk,bhkd->bhgqd', probs, v)
        out = out.reshape(bsz, HEADS, q_len, HEAD_DIM).transpose(0, 2, 1, 3)
        out = out.reshape(bsz, q_len, HEADS * HEAD_DIM)
        return out @ Wo

    def _L2_ffn_ref(x, w1, s1, w2, s2, w3, s3):
        import jax, jax.numpy as jnp
        import numpy as np
        GROUP = 64

        def dequant_q40(w, s, out_features, in_features):
            msb = w >> 4
            lsb = (w & 15 ^ 8) - 8
            g = jnp.concatenate([msb, lsb], axis=1).reshape(-1, GROUP)
            deq = g.astype(s.dtype) * s[:, None]
            return deq.reshape(out_features, in_features)
        dim = x.shape[-1]
        hidden = w1.shape[0] * w1.shape[1] * 2 // dim
        W1 = dequant_q40(w1, s1, hidden, dim)
        W3 = dequant_q40(w3, s3, hidden, dim)
        W2 = dequant_q40(w2, s2, dim, hidden)
        a = jnp.einsum('bsd,hd->bsh', x, W1)
        b = jnp.einsum('bsd,hd->bsh', x, W3)
        h = jax.nn.silu(a) * b
        return jnp.einsum('bsh,dh->bsd', h, W2)

    def _L3_xattn_ref(text, features, Wq, bq, Wk, bk):
        import jax, jax.numpy as jnp
        import numpy as np
        TEXT_DIM = 512
        FEATURE_DIM = 512

        def _xavier_uniform(key, shape):
            fan_in, fan_out = (shape[1], shape[0])
            limit = float(np.sqrt(6.0 / (fan_in + fan_out)))
            return jax.random.uniform(key, shape, jnp.float32, -limit, limit)
        Q = jnp.einsum('btx,dx->btd', text, Wq) + bq
        K = jnp.einsum('bpx,dx->bpd', features, Wk) + bk
        scale = 1.0 / jnp.sqrt(jnp.asarray(K.shape[-1], K.dtype))
        scores = jnp.einsum('btd,bpd->btp', Q, K) * scale
        attn = jax.nn.softmax(scores, axis=-1)
        attended = jnp.einsum('btp,bpd->btd', attn, features)
        return attended

    def _L3_ffn_ref(hidden_states, router_weight, router_bias, expert_bias):
        import jax, jax.numpy as jnp
        import numpy as np
        K_TOP = 8
        B, S, H = hidden_states.shape
        E = router_weight.shape[0]
        T = B * S
        flat = hidden_states.reshape(T, H)
        logits = jnp.einsum('th,eh->te', flat, router_weight) + router_bias
        scores = jax.nn.softmax(logits, axis=-1)
        topk_w, topk_idx = jax.lax.top_k(scores, K_TOP)
        w_sum = topk_w.sum(axis=-1, keepdims=True)
        w_dense = jnp.zeros((T, E), dtype=scores.dtype).at[jnp.arange(T)[:, None], topk_idx].add(topk_w)
        bias_mix = jnp.einsum('te,eh->th', w_dense, expert_bias)
        out = flat * w_sum + bias_mix
        return out.reshape(B, S, H)
    x = x + _L0_xattn_ref(_layernorm(x, axis=-1), ctx_4096, L0_xattn_x1_scale, L0_xattn_x1_zp, L0_xattn_x2_scale, L0_xattn_x2_zp)
    x = x + _L0_ffn_ref(_layernorm(x, axis=-1), L0_ffn_gate_w, L0_ffn_up_w, L0_ffn_down_w, L0_ffn_gate_scale, L0_ffn_up_scale, L0_ffn_down_scale)
    x = x + _L1_xattn_ref(_layernorm(x, axis=-1), ctx_4096, L1_xattn_Wq, L1_xattn_Wk, L1_xattn_Wv, L1_xattn_Wo)
    x = x + _L1_ffn_ref(_layernorm(x, axis=-1), L1_ffn_gate_w, L1_ffn_expert_w)
    x = x + _L2_xattn_ref(_layernorm(x, axis=-1), ctx_4096, L2_xattn_Wq, L2_xattn_Wk, L2_xattn_Wv, L2_xattn_Wo, L2_xattn_q_norm_w, L2_xattn_k_norm_w)
    x = x + _L2_ffn_ref(_layernorm(x, axis=-1), L2_ffn_w1, L2_ffn_s1, L2_ffn_w2, L2_ffn_s2, L2_ffn_w3, L2_ffn_s3)
    x = x + _L3_xattn_ref(_layernorm(x, axis=-1), ctx_4096, L3_xattn_Wq, L3_xattn_bq, L3_xattn_Wk, L3_xattn_bk)
    x = x + _L3_ffn_ref(_layernorm(x, axis=-1), L3_ffn_router_weight, L3_ffn_router_bias, L3_ffn_expert_bias)
    return x

_drawn_inputs = setup_inputs


def setup_inputs(seed=0):
    import zlib

    import numpy as np

    out = dict(_drawn_inputs(seed))
    spreads = {'L2_xattn_q_norm_w': (1.0, 0.6),
     'L2_xattn_k_norm_w': (1.0, 0.6),
     'L3_xattn_bq': (0.0, 2.0),
     'L3_xattn_bk': (0.0, 2.0),
     'L3_ffn_router_bias': (0.0, 2.0)}
    factors = {'L0_ffn_gate_w': 8.0,
     'L0_ffn_up_w': 8.0,
     'L0_ffn_down_w': 8.0,
     'L1_ffn_gate_w': 3.884,
     'L1_ffn_expert_w': 3.437,
     'L2_xattn_Wq': 8.0,
     'L2_xattn_Wk': 8.0,
     'L2_xattn_Wv': 5.044,
     'L2_xattn_Wo': 5.123,
     'L2_ffn_s1': 2.99,
     'L2_ffn_s2': 3.1,
     'L2_ffn_s3': 3.125,
     'L3_xattn_Wq': 16.054,
     'L3_xattn_Wk': 15.353,
     'L3_ffn_router_weight': 32.597,
     'L3_ffn_expert_bias': 32.252,
     'L1_xattn_Wq': 3.159,
     'L1_xattn_Wk': 3.193}
    for name, (base, spread) in spreads.items():
        noise = np.random.default_rng([zlib.crc32(name.encode()), seed]).standard_normal(out[name].shape)
        drawn = base * np.exp(spread * noise) if base else spread * noise
        out[name] = jnp.asarray(drawn.astype(out[name].dtype))
    for name, factor in factors.items():
        out[name] = (out[name] * factor).astype(out[name].dtype)
    return out
```

```python
from collections import Counter
from contextlib import ExitStack

import concourse.bass as bass
from concourse import mybir

F32 = mybir.dt.float32
F32R = mybir.dt.float32r
BF16 = mybir.dt.bfloat16
I32 = mybir.dt.int32
ALU = mybir.AluOpType
ACT = mybir.ActivationFunctionType
AX = mybir.AxisListType

P = 128
B, SQ, D = 2, 256, 512
SC = 512
KT = D // P
TT = B * SQ // P
KV = SC + SQ
KVT = KV // P
HD = 128
HEADS = 32
INTER = 1376
IT = -(-INTER // P)
EXPERTS = 8
ROUTED, RTOP = 64, 8
GROUP = 64
ROUND = 1.5 * 2.0 ** 23
MID = 128.0
BIG = 3.0e38

LAYER = {1: dict(kv=4, pairs=4, rms=False), 2: dict(kv=8, pairs=2, rms=True)}


def adds(step):
    k = step[0]
    if k == "W":
        ring = RINGS[step[1]]
        return {step[2]: 16, "hi_" + ring: 1, "lo_" + ring: 1}
    if k == "K":
        return {"g_full": 1, "g_done": 1, "k_sq" if step[2] else "hi": 1}
    if k == "KN":
        return {"g_full": 1, "g_done": 1, "k_ln": 1, "k_r": 1}
    if k == "KM":
        return {"k_raw": 1, "hi": 1, "k_lo": 1}
    if k == "q":
        return {"g_full": 1, "g_done": 1, "hi": 1, **({"q_sq": 1} if step[3] else {})}
    if k == "QN":
        return {"g_full": 1, "g_done": 1, "rq": 1}
    if k in ("PV", "cq", "ck"):
        return {"g_full": 1, "g_done": 1, "hi": 1}
    if k in ("V", "Wo", "E", "gate", "qmm", "cpv", "rl", "rm"):
        return {"g_full": 1, "g_done": 1}
    if k in ("VT", "xnT", "ct", "rt"):
        return {"t_full": 1, "t_done": 1, "hi": 1}
    if k == "xqT":
        return {"t_full": 1, "t_done": 1}
    if k == "TW":
        return {"t_full": 1, "t_done": 1, "hi": 1}
    if k == "cut":
        return {"cut": 1}
    if k == "S":
        return {"s_full": 1, "s_max": 1, "bias": 1}
    if k == "X":
        return {"exp": 1}
    if k == "R":
        return {"rinv": 1, "p_ready": 1}
    if k == "T":
        return {"t_full": 2, "t_done": 2, "hi": 2}
    if k == "GU":
        return {"g_full": 2, "g_done": 2, "silu": 1, "hi": 1, "inner": 1}
    if k == "D":
        return {"d_full": 1}
    if k == "DQ":
        return {f"dma_w13_{step[1] % 2}": 32, "nib": 1, "dq": 1}
    return {}


RINGS = {"gu0": "gu", "gu1": "gu", "dn0": "dn", "dn1": "dn", "kv": "rq", "q": "rq", "o": "o", "e0": "e", "e1": "e"}


class Counts:

    def __init__(self):
        self.base, self.here = Counter(g_done=2, t_done=2), Counter()
        self.per, self.turn = Counter(), None

    def any(self, sem, more=0):
        return self.base[sem] + self.here[sem] + more > 0

    def at(self, sem, more=0):
        v = self.base[sem] + self.here[sem] + more
        return v if self.turn is None or not self.per[sem] else self.turn * self.per[sem] + v

    def even(self, sem, more=0):
        assert self.turn is None or self.per[sem] % 2 == 0, sem
        return (self.base[sem] + self.here[sem] + more) % 2

    def enter(self, turn, steps):
        self.base.update(self.here)
        self.here, self.turn, self.per = Counter(), turn, Counter()
        for s in steps:
            self.per.update(adds(s))

    def leave(self, turns):
        assert +self.here == +self.per, (self.here, self.per)
        for k, v in self.per.items():
            self.base[k] += v * turns
        self.here, self.turn, self.per = Counter(), None, Counter()


def ln_steps():
    return [("stats",), *[("xnT", tt) for tt in range(TT)]]


def ffn_segments(quantised):
    def w(name, i, per=0):
        slot = f"{name}{i % 2}"
        return [("W", slot, "dma_" + slot, i, per)] if i < IT else []

    def dq(i, per=0):
        return [("DQ", i, per)] if i < IT else []

    def cut(i, per=0):
        return [("cut", i, per)] if i < IT else []

    def tw(which, i, per=0):
        return [("TW", which, i, per)] if i < IT else []

    if not quantised:
        first = [*w("gu", 0), *w("dn", 0), *w("gu", 1), ("zeroY",), ("GU", 0), *w("gu", 2), *w("dn", 1)]

        def body(i, per):
            out = []
            for j in (i, i + 1):
                out += [("GU", j + 1), *w("gu", j + 3, per), ("D", j), *w("dn", j + 2, per)]
            return out
    else:
        first = [("DQ", 0, 0), ("TW", 0, 0, 0), ("TW", 1, 0, 0), ("DQ", 1, 0), ("zeroY",), ("GU", 0), ("TW", 0, 1, 0),
                 ("TW", 1, 1, 0), ("DQ2",), ("cut", 0, 0), ("TW", 2, 0, 0), ("cut", 1, 0), ("TW", 2, 1, 0), ("DQ", 2, 0)]

        def body(i, per):
            out = []
            for j in (i, i + 1):
                out += [("GU", j + 1), *cut(j + 2, per), *tw(0, j + 2, per), *tw(1, j + 2, per), ("D", j),
                        *tw(2, j + 2, per), *dq(j + 3, per)]
            return out
    n = (IT - 1) // 2 - 1
    return [(1, first), (n, body(0, 2)), (1, body(2 * n, 0) + [("D", IT - 1), ("Yadd", quantised)])]


def attention_segments(layer):
    n_kv, pairs, rms = LAYER[layer]["kv"], LAYER[layer]["pairs"], LAYER[layer]["rms"]
    units = 8 * pairs

    def turn(first, per, more):
        def chunk(j, kind):
            return first + (j // pairs) * (1 + 2 * pairs) + kind + 2 * (j % pairs)

        def wkv():
            return [("W", "kv", "dma_rq", first + 1 + 2 * pairs, per)] if more else []

        def wq(j):
            return [("W", "q", "dma_rq", chunk(j, 1), per)] if more or j < pairs else []

        def wo(j):
            return [("W", "o", "dma_ro", chunk(j, 2), per)] if more or j < pairs else []

        def q(j, h):
            return [("q", j, h, rms)] if more or j < pairs else []

        def qn(j):
            return [("QN", j)] if rms and (more or j < pairs) else []

        def k(n):
            return [("K", n, rms)] if more else []

        def kn(n):
            return [("KN", n)] if rms and more else []

        def km(n):
            return [("KM", n)] if rms and more else []

        out = [("V", 0), ("S", 0), ("V", 1), ("X", 0), ("S", 1), ("VT", 0), ("R", 0), ("X", 1), ("V", 2), ("R", 1), ("VT", 1)]
        for u in range(units - 2):
            j, r = divmod(u, 8)
            if u in (1, 2):
                out += [("VT", u + 1)]
            out += [("S", u + 2), ("T", u), ("X", u + 2)]
            if u == 0:
                out += [("V", 3), *wkv()]
            elif r == 0:
                out += [("PV", 2 * j - 1)]
            elif r == 1 and j:
                out += [("Wo", 2)]
            elif r == 2 and j:
                out += [("Wo", 3), *wo(j)]
            elif r == 3:
                out += q(j + 1, 0)
            elif r == 4:
                out += [*q(j + 1, 1), *wq(j + 2)]
            elif r == 5:
                out += [*qn(j + 1), ("PV", 2 * j)]
            elif r > 5:
                out += [("Wo", r - 6)]
            out += [("R", u + 2)]
        return out + [("T", units - 2), *k(0), ("Wo", 0), *k(1), *kn(0), ("T", units - 1), ("Wo", 1), *km(0),
                      *k(2), *kn(1), *km(1), *k(3), *kn(2), ("PV", 2 * pairs - 1), *km(2), *kn(3), ("Wo", 2), *km(3),
                      ("Wo", 3), *wo(pairs)]

    per = 1 + 2 * pairs
    first = [("W", "kv", "dma_rq", 0, 0), ("W", "q", "dma_rq", 1, 0), ("W", "o", "dma_ro", 2, 0)]
    for n in range(4):
        if rms and n > 1:
            first += [("KM", n - 2)]
        first += [("K", n, rms)]
        if rms and n:
            first += [("KN", n - 1)]
    first += [("q", 0, 0, rms), *([("KM", 2), ("KN", 3)] if rms else []), ("q", 0, 1, rms),
              *([("KM", 3)] if rms else []), ("W", "q", "dma_rq", 3, 0)]
    if rms:
        first += [("QN", 0)]
    return [(1, first), (n_kv - 1, turn(0, per, True)), (1, turn((n_kv - 1) * per, 0, False))]


def experts_segments():
    def w(e, per=0):
        return [("W", f"e{e % 2}", f"dma_e{e % 2}", e, per)] if e < EXPERTS else []

    def pair(e, per):
        out = []
        for x in (e, e + 1):
            out += [*[("E", x, tt, per) for tt in range(TT)], *w(x + 2, per)]
        return out
    n = EXPERTS // 2 - 1
    return [(1, [*w(0), *w(1), *[("gate", tt) for tt in range(TT)]]),
            (n, pair(0, 2)), (1, pair(2 * n, 0))]


def cross_steps():
    out = [("cq", dt) for dt in range(KT)] + [("ck", b, dt) for b in range(B) for dt in range(KT)]
    out += [("cs", 0), ("cs", 1)]
    for tt in range(TT):
        out += [("ct", tt), *([("cs", tt + 2)] if tt + 2 < TT else []), ("cpv", tt)]
    return out


def router_steps():
    out = [("rl", tt) for tt in range(TT)]
    for tt in range(TT):
        out += [("rt", tt), ("rm", tt)]
    return out


def segments(blocks):
    out = [[(1, [("start",), ("stats",), *[("xqT", tt) for tt in range(TT)], ("sums",), *[("qmm", tt) for tt in range(TT)]])],
           [(1, ln_steps()), *ffn_segments(False)],
           [(1, ln_steps()), *attention_segments(1)],
           [(1, ln_steps()), *experts_segments()],
           [(1, ln_steps()), *attention_segments(2)],
           [(1, ln_steps()), *ffn_segments(True)],
           [(1, ln_steps()), (1, cross_steps())],
           [(1, ln_steps()), (1, router_steps())]]
    return out[:blocks]


def build_program(nc, ins, out, blocks=8):
    ctx = ExitStack()
    with ctx:
        sems = {}

        def sem(name):
            if name not in sems:
                sems[name] = ctx.enter_context(nc.semaphore(name))
            return sems[name]

        def sb(scope, name, shape, dt=F32):
            return scope.enter_context(nc.sbuf_tensor(name, shape, dt))

        def pair(scope, name, shape):
            return (sb(scope, name + "_hi", shape, F32R), sb(scope, name + "_lo", shape, F32R))

        X = sb(ctx, "X", [P, TT, D])
        H = pair(ctx, "H", [P, KT, B, KV])
        ident = sb(ctx, "ident", [P, P])
        ones = sb(ctx, "ones", [P, P])
        zeros_bf = sb(ctx, "zeros_bf", [P, D], BF16)
        ones_bf = sb(ctx, "ones_bf", [P, P], BF16)
        neg_half = sb(ctx, "neg_half", [P, 8])
        small = sb(ctx, "small", [P, 7])
        moments = sb(ctx, "moments", [P, TT, 6])
        mean_var = sb(ctx, "mean_var", [P, TT, 2])
        var = sb(ctx, "var", [P, TT])
        rstd = sb(ctx, "rstd", [P, TT])

        with ExitStack() as scope:
            xn = sb(scope, "xn", [P, TT, D])
            ctx_raw = sb(scope, "ctx_raw", [P, B * SC // P, D])
            ctxT_raw = sb(scope, "ctxT_raw", [P, KT, B, SC])
            ctx_q = sb(scope, "ctx_q", [P, B * SC // P, D], BF16)
            xq_T = sb(scope, "xq_T", [P, KT, TT * P], BF16)
            derived = sb(scope, "derived", [P, 8])
            cz = sb(scope, "cz", [P, B, D])
            row_bias = sb(scope, "row_bias", [P, TT])
            q_tmp = sb(scope, "q_tmp", [P, D])
            inner0 = [pair(scope, f"inner0{i}", [P, TT * P]) for i in range(2)]
            gated0 = sb(scope, "gated0", [P, TT * P])
            silu0 = sb(scope, "silu0", [P, TT * P])
            gu_raw = [sb(scope, f"gu_raw{i}", [P, 2 * KT * P]) for i in range(2)]
            dn_raw = [sb(scope, f"dn_raw{i}", [P, D]) for i in range(2)]
            gu0 = [pair(scope, f"gu{i}", [P, 2 * KT * P]) for i in range(2)]
            dn0 = [pair(scope, f"dn{i}", [P, D]) for i in range(2)]

        with ExitStack() as scope:
            PT = [pair(scope, f"PT{i}", [P, KVT, 4 * P]) for i in range(2)]
            KX = pair(scope, "KX", [P, B * KV])
            VX = pair(scope, "VX", [P, B * KVT, HD])
            vT = [sb(scope, f"vT{i}", [P, 3 * P]) for i in range(2)]
            k_raw = [*vT, *[sb(scope, f"k_raw{i}", [P, 3 * P]) for i in range(2)]]
            prob = [sb(scope, f"prob{i}", [P, KV]) for i in range(2)]
            QX = [pair(scope, f"QX{i}", [P, 2, TT * P]) for i in range(2)]
            OX = pair(scope, "OX", [P, 2, TT * P])
            raw_q = sb(scope, "raw_q", [P, 1024])
            raw_o = sb(scope, "raw_o", [P, 1024])
            w_kv = pair(scope, "w_kv", [P, 1024])
            w_q = pair(scope, "w_q", [P, 1024])
            w_o = pair(scope, "w_o", [P, 1024])
            q_sq = [sb(scope, f"q_sq{i}", [P, TT * P]) for i in range(2)]
            k_sq = [t[:, 0:3 * P] for t in q_sq]
            k_r = [sb(scope, f"k_r{i}", [P, 3 * P]) for i in range(2)]
            top = sb(scope, "top", [P, 4])
            nbias = sb(scope, "nbias", [P, 4])
            rsum = sb(scope, "rsum", [P, 4])
            rinv = sb(scope, "rinv", [P, 4])
            qvar = sb(scope, "qvar", [P, 8])
            rq = [sb(scope, f"rq{i}", [P, 8]) for i in range(2)]
            qk_w = sb(scope, "qk_w", [P, 3])
        with ExitStack() as scope:
            sb(scope, "pad1", [P, TT, D])
            gate_raw = sb(scope, "gate_raw", [P, KT, EXPERTS])
            gate_w = pair(scope, "gate_w", [P, KT, EXPERTS])
            WIDE = EXPERTS + 6
            padded = sb(scope, "padded", [P, TT, WIDE])
            top8 = sb(scope, "top8", [P, TT, 8])
            left = sb(scope, "left", [P, TT, WIDE])
            chosen = sb(scope, "chosen", [P, TT, EXPERTS])
            ntop = sb(scope, "ntop", [P, TT])
            e_exp = sb(scope, "e_exp", [P, TT, EXPERTS])
            e_sum = sb(scope, "e_sum", [P, TT])
            e_inv = sb(scope, "e_inv", [P, TT])
            e_w = sb(scope, "e_w", [P, TT, EXPERTS])
            ex_raw = [sb(scope, f"ex_raw{i}", [P, KT * D]) for i in range(2)]
            ex_w = [pair(scope, f"ex_w{i}", [P, KT * D]) for i in range(2)]

        with ExitStack() as scope:
            inner2 = [pair(scope, f"inner2{i}", [P, TT * P]) for i in range(2)]
            gated2 = sb(scope, "gated2", [P, TT * P])
            silu2 = sb(scope, "silu2", [P, TT * P])
            gu2 = [pair(scope, f"gu2{i}", [P, 2 * KT * P]) for i in range(2)]
            dn2 = [pair(scope, f"dn2{i}", [P, D]) for i in range(2)]
            w2_raw = sb(scope, "w2_raw", [P, 43, GROUP], I32)
            w2_s = sb(scope, "w2_s", [P, 43, 2])
            w2_nib = sb(scope, "w2_nib", [P, 43, GROUP], I32)
            w2_nat = sb(scope, "w2_nat", [P, 4 * INTER + P])
            w2_cut = sb(scope, "w2_cut", [P, 4, P])
            w13_raw = [sb(scope, f"w13_raw{i}", [P, 2 * KT, GROUP], I32) for i in range(2)]
            w13_s = [sb(scope, f"w13_s{i}", [P, 2 * KT, 2]) for i in range(2)]
            w13_nib = [sb(scope, f"w13_nib{i}", [P, 2 * KT, GROUP], I32) for i in range(2)]
            w13_nat = sb(scope, "w13_nat", [P, 2 * KT, 2, GROUP])

        with ExitStack() as scope:
            QC = pair(scope, "QC", [P, KT, TT * P])
            c_raw = sb(scope, "c_raw", [P, B * SC // P, D])
            c_w = pair(scope, "c_w", [P, B * SC // P, D])
            x_w = [pair(scope, f"x_w{i}", [P, KT * D]) for i in range(2)]
            KC = pair(scope, "KC", [P, KT, B * SC])
            stat_c = sb(scope, "stat_c", [P, 4, TT])
            bias_c = sb(scope, "bias_c", [P, 2, KT])
            with ExitStack() as inner_scope:
                x_raw = [sb(inner_scope, f"x_raw{i}", [P, KT * D]) for i in range(2)]
            prob_c = [sb(scope, f"prob_c{i}", [P, SC]) for i in range(2)]
            PC = [pair(scope, f"PC{i}", [P, SC // P, P]) for i in range(2)]

        with ExitStack() as scope:
            sb(scope, "pad4", [P, TT, D])
            r_raw = sb(scope, "r_raw", [P, KT, ROUTED])
            r_w = pair(scope, "r_w", [P, KT, ROUTED])
            r_bias = sb(scope, "r_bias", [P, ROUTED])
            eb_raw = sb(scope, "eb_raw", [ROUTED, D])
            eb_w = pair(scope, "eb_w", [ROUTED, D])
            r_log = sb(scope, "r_log", [P, TT, ROUTED])
            r_exp = sb(scope, "r_exp", [P, TT, ROUTED])
            r_sc = sb(scope, "r_sc", [P, TT, ROUTED])
            r_left = sb(scope, "r_left", [P, TT, ROUTED])
            r_dense = sb(scope, "r_dense", [P, TT, ROUTED])
            r_top = sb(scope, "r_top", [P, TT, 8])
            r_stat = sb(scope, "r_stat", [P, 5, TT])
            r_T = [pair(scope, f"r_T{i}", [ROUTED, P]) for i in range(2)]
            r_y = sb(scope, "r_y", [P, TT, D])

        banks = ctx.enter_context(nc.psum_tensor("banks", [P, 8, 512], F32))
        flat = banks[:, :, :].rearrange("p b n -> p (b n)")
        S = [flat[:, 1024 * i:1024 * i + KV] for i in range(2)]
        Y = [banks[:, i, :] for i in range(4)]
        T = [banks[:, 4 + i, :] for i in range(2)]
        G = [banks[:, 6 + i, :] for i in range(2)]

        slots = {"gu0": (gu_raw[0], gu0[0], "w_ffn0", (0, 1024)), "gu1": (gu_raw[1], gu0[1], "w_ffn0", (0, 1024)),
                 "dn0": (dn_raw[0], dn0[0], "w_ffn0", (1024, 1536)), "dn1": (dn_raw[1], dn0[1], "w_ffn0", (1024, 1536)),
                 "kv": (raw_q, w_kv, None, (0, 1024)), "q": (raw_q, w_q, None, (0, 1024)),
                 "o": (raw_o, w_o, None, (0, 1024)),
                 "e0": (ex_raw[0], ex_w[0], "w_experts", (0, 2048)), "e1": (ex_raw[1], ex_w[1], "w_experts", (0, 2048))}

        def latents(h, kt, tt):
            return h[:, kt, tt // 2, SC + (tt % 2) * P:SC + (tt % 2) * P + P]

        def all_latents(h, kt):
            return h[:, kt, :, SC:KV]

        def keys(h, kt, n):
            return h[:, kt, n // 2, 384 * (n % 2):384 * (n % 2) + 384]

        def latents_all(h, tt):
            return h[:, :, tt // 2, SC + (tt % 2) * P:SC + (tt % 2) * P + P]

        def turned_weights(which, i, part, bank):
            if which < 2:
                dst = gu2[i % 2][part][:, :].rearrange("p (k n) -> p k n", k=KT)[:, :, which * P:which * P + P]
                return dst, bank.rearrange("p (k n) -> p k n", k=KT)
            return dn2[i % 2][part][:, :].rearrange("p (m r) -> p r m", r=4), bank.rearrange("p (r m) -> p r m", r=4)

        def crossed(step, part):
            if step[0] == "cq":
                return QC[part][:, step[1], :], bias_c[:, 0, step[1]:step[1] + 1]
            _, b, dt = step
            return KC[part][:, dt, b * SC:b * SC + SC], bias_c[:, 1, dt:dt + 1]

        def f32(ap):
            return ap.bitcast(F32)

        small_names = {n: i for i, n in enumerate(("s1", "z1", "s2", "z2", "gate", "up", "down"))}

        def sc(name):
            i = small_names[name]
            return small[:, i:i + 1]

        def units_of(number):
            return 8 * LAYER[number // 2]["pairs"]

        def walk(c, eng, do):
            for number, block in enumerate(segments(blocks)):
                for turns, steps in block:
                    if turns == 1:
                        for s in steps:
                            do(s, number, None)
                            c.here.update(adds(s))
                    else:
                        with eng.Fori(0, turns) as turn:
                            c.enter(turn, steps)
                            for s in steps:
                                do(s, number, turn)
                                c.here.update(adds(s))
                        c.leave(turns)

        block = ctx.enter_context(nc.Block())

        @block.sync
        def _(sp):
            c = Counts()
            stores = 0

            def row(i, per, turn):
                return i if turn is None else sp.snap(turn * per + i)

            def chunk(dram, at, lo, hi):
                return dram[bass.ds(at, 1), :, lo:hi].rearrange("a p n -> (a p) n")

            def do(step, number, turn):
                k = step[0]
                if k == "start":
                    sp.dma_start(X[:, :, :], ins["x"].rearrange("b (t p) d -> p (b t) d", p=P)).then_inc(sem("dma_x"), 16)
                    sp.dma_start(small[:, :], ins["small"]).then_inc(sem("dma_small"), 16)
                    sp.dma_start(ctx_raw[:, :, :], ins["ctx"].rearrange("b (t p) d -> p (b t) d", p=P)).then_inc(sem("dma_ctx"), 16)
                    sp.dma_start(ctxT_raw[:, :, :, :], ins["ctxT"]).then_inc(sem("dma_ctxT"), 16)
                elif k == "stats" and number >= 2:
                    sp.wait_ge(sem("rstd"), number + 1)
                    if number == 4:
                        sp.dma_start(qk_w[:, 0:2], ins["qk_norm"]).then_inc(sem("dma_qk"), 16)
                    if number == 3:
                        sp.dma_start(gate_raw[:, :, :], ins["gate_w"]).then_inc(sem("dma_gate"), 16)
                    if number == 5:
                        sp.dma_start(w2_raw[:, :, :], ins["w2"]).then_inc(sem("dma_w2"), 16)
                        sp.dma_start(w2_s[:, :, :], ins["s2"]).then_inc(sem("dma_w2"), 16)
                    if number == 6:
                        sp.dma_start(x_raw[0][:, :], ins["w_cross"][0]).then_inc(sem("dma_xq"), 16)
                        sp.dma_start(bias_c[:, :, :], ins["b_cross"]).then_inc(sem("dma_bc"), 16)
                        sp.dma_start(x_raw[1][:, :], ins["w_cross"][1]).then_inc(sem("dma_xk"), 16)
                        sp.dma_start(c_raw[:, :, :], ins["ctx"].rearrange("b (t p) d -> p (b t) d", p=P)).then_inc(sem("dma_c"), 16)
                    if number == 7:
                        sp.dma_start(r_raw[:, :, :], ins["router_w"]).then_inc(sem("dma_r"), 16)
                        sp.dma_start(r_bias[:, :], ins["router_b"]).then_inc(sem("dma_rb"), 16)
                        sp.dma_start(eb_raw[:, :], ins["expert_b"]).then_inc(sem("dma_eb"), 16)
                elif k == "W":
                    _, slot, dma, i, per = step
                    raw, _, dram, (lo, hi) = slots[slot]
                    dram = ins[dram or ("w_attn1" if number == 2 else "w_attn2")]
                    ring = RINGS[slot]
                    at = row(i, per, turn)
                    if slot in ("kv", "q"):
                        if c.any("lo_rq"):
                            sp.wait_ge(sem("lo_rq"), c.at("lo_rq"))
                    else:
                        back = -1 if ring in ("gu", "dn", "e") else 0
                        if c.any("lo_" + ring, back):
                            sp.wait_ge(sem("lo_" + ring), c.at("lo_" + ring, back))
                    sp.dma_start(raw[:, :], chunk(dram, at, lo, hi)).then_inc(sem(dma), 16)
                elif k == "DQ":
                    _, i, per = step
                    at = row(i, per, turn)
                    if c.any("dq", -1):
                        sp.wait_ge(sem("dq"), c.at("dq", -1))
                    d = sem(f"dma_w13_{i % 2}")
                    sp.dma_start(w13_raw[i % 2][:, :, :].rearrange("p a g -> p (a g)"),
                                 ins["w13"][bass.ds(at, 1)].rearrange("a p n -> (a p) n")).then_inc(d, 16)
                    sp.dma_start(w13_s[i % 2][:, :, :].rearrange("p a g -> p (a g)"),
                                 ins["s13"][bass.ds(at, 1)].rearrange("a p n -> (a p) n")).then_inc(d, 16)

            walk(c, sp, do)
            sp.wait_ge(sem("result"), 1)
            sp.dma_start(out.rearrange("b (t p) d -> p (b t) d", p=P), X[:, :, :]).then_inc(sem("dma_out"), 16)
            sp.wait_ge(sem("dma_out"), 16)

        @block.tensor
        def _(pe):
            c = Counts()

            def mm3(o, a, b, start, stop):
                nc.tensor.matmul(o, a[0], b[0], start=start, stop=False)
                nc.tensor.matmul(o, a[0], b[1], start=False, stop=False)
                return nc.tensor.matmul(o, a[1], b[0], start=False, stop=stop)

            heads_out = [None]

            def over(pair_, f):
                return tuple(f(t) for t in pair_)

            def do(step, number, turn):
                k = step[0]
                if k in ("xnT", "xqT"):
                    tt = step[1]
                    if tt == 0:
                        pe.wait_ge(sem("const"), 1)
                    pe.wait_ge(sem("xn"), TT * number + tt + 1)
                    pe.wait_ge(sem("t_done"), c.at("t_done", -1))
                    t = T[c.even("t_full")]
                    for kt in range(KT):
                        m = nc.tensor.transpose(t[:, kt * P:kt * P + P], xn[:, tt, kt * P:kt * P + P], ident[:, :])
                    m.then_inc(sem("t_full"), 1)
                elif k == "sums":
                    pe.wait_ge(sem("cq"), 1)
                    for b in range(B):
                        for kt in range(SC // P):
                            m = nc.tensor.matmul(Y[b], ones_bf[:, :], ctx_q[:, b * 4 + kt, :], start=kt == 0, stop=kt == 3)
                    m.then_inc(sem("csum"), 1)
                    pe.wait_ge(sem("t_done"), c.at("t_done"))
                    for tt in range(TT):
                        for kt in range(KT):
                            m = nc.tensor.matmul(Y[2][:, 2 * tt:2 * tt + 2], xq_T[:, kt, tt * P:tt * P + P],
                                                 ones_bf[:, 0:2], start=kt == 0, stop=kt == KT - 1)
                    m.then_inc(sem("rowsum"), 1)
                elif k == "qmm":
                    tt = step[1]
                    pe.wait_ge(sem("g_done"), c.at("g_done", -1))
                    g = G[c.even("g_full")]
                    for kt in range(KT):
                        m = nc.tensor.matmul(g, xq_T[:, kt, tt * P:tt * P + P], ctx_q[:, (tt // 2) * 4 + kt, :],
                                             start=kt == 0, stop=kt == KT - 1)
                    m.then_inc(sem("g_full"), 1)
                elif k == "zeroY":
                    for tt in range(TT):
                        nc.tensor.matmul(Y[tt], zeros_bf[:, 0:P], zeros_bf[:, :], start=True, stop=False)
                elif k == "GU":
                    i = step[1]
                    w = gu0[i % 2] if number == 1 else gu2[i % 2]
                    if number == 1:
                        pe.wait_ge(sem("lo_gu"), c.at("lo_gu", i + 1 - min(i + 2, IT)))
                        if i == 0:
                            pe.wait_ge(sem("t_done"), c.at("t_done"))
                    else:
                        pe.wait_ge(sem("t_done"), c.at("t_done", 0 if i == 0 else -1))
                    for job, off in ((0, 0), (1, P)):
                        pe.wait_ge(sem("g_done"), c.at("g_done", job - 1))
                        g = G[c.even("g_full", job)]
                        for kt in range(KT):
                            a = over(w, lambda t: t[:, kt * 256 + off:kt * 256 + off + P])
                            m = mm3(g, a, over(H, lambda h: all_latents(h, kt)), kt == 0, kt == KT - 1)
                        m.then_inc(sem("g_full"), 1)
                elif k == "D":
                    i = step[1]
                    w = dn0[i % 2] if number == 1 else dn2[i % 2]
                    pe.wait_ge(sem("inner"), c.at("inner", 0 if i == IT - 1 else -1))
                    if number == 1:
                        pe.wait_ge(sem("lo_dn"), c.at("lo_dn", i + 1 - min(i + 2, IT)))
                    elif i == IT - 1:
                        pe.wait_ge(sem("t_done"), c.at("t_done"))
                    for tt in range(TT):
                        m = mm3(Y[tt], over(inner0[i % 2] if number == 1 else inner2[i % 2], lambda t: t[:, tt * P:tt * P + P]),
                                over(w, lambda t: t[:, :]), False, i == IT - 1)
                    m.then_inc(sem("d_full"), 1)
                elif k == "K":
                    n = step[1]
                    if n == 0:
                        pe.wait_ge(sem("lo_rq"), c.at("lo_rq"))
                        if turn is None:
                            pe.wait_ge(sem("ctx_lo"), KT)
                            pe.wait_ge(sem("t_done"), c.at("t_done"))
                    pe.wait_ge(sem("g_done"), c.at("g_done", -1))
                    g = G[c.even("g_full")]
                    for kt in range(KT):
                        m = mm3(g[:, 0:384], over(w_kv, lambda t: t[:, kt * 256:kt * 256 + P]),
                                over(H, lambda h: keys(h, kt, n)), kt == 0, kt == KT - 1)
                    m.then_inc(sem("g_full"), 1)
                elif k == "KN":
                    n = step[1]
                    pe.wait_ge(sem("k_sq"), c.at("k_sq", 0 if n == 3 else -1))
                    pe.wait_ge(sem("g_done"), c.at("g_done", -1))
                    g = G[c.even("g_full")]
                    nc.tensor.matmul(g[:, 0:384], ones[:, :], k_sq[n % 2], start=True, stop=True)\
                        .then_inc(sem("g_full"), 1)
                elif k == "q":
                    _, j, h, rms = step
                    if h == 0:
                        pe.wait_ge(sem("lo_rq"), c.at("lo_rq"))
                    pe.wait_ge(sem("g_done"), c.at("g_done", -1))
                    g = G[c.even("g_full")]
                    for kt in range(KT):
                        m = mm3(g, over(w_q, lambda t: t[:, kt * 256 + h * P:kt * 256 + h * P + P]),
                                over(H, lambda t: all_latents(t, kt)), kt == 0, kt == KT - 1)
                    m.then_inc(sem("g_full"), 1)
                elif k == "QN":
                    pe.wait_ge(sem("q_sq"), c.at("q_sq"))
                    pe.wait_ge(sem("g_done"), c.at("g_done", -1))
                    g = G[c.even("g_full")]
                    for i in range(8):
                        m = nc.tensor.matmul(g[:, i:i + 1], q_sq[i // 4][:, (i % 4) * P:(i % 4) * P + P], ones[:, 0:1],
                                             start=True, stop=True)
                    m.then_inc(sem("g_full"), 1)
                elif k == "V":
                    n = step[1]
                    pe.wait_ge(sem("g_done"), c.at("g_done", -1))
                    g = G[c.even("g_full")]
                    for kt in range(KT):
                        m = mm3(g[:, 0:384], over(w_kv, lambda t: t[:, kt * 256 + P:kt * 256 + 2 * P]),
                                over(H, lambda h: keys(h, kt, n)), kt == 0, kt == KT - 1)
                    m.then_inc(sem("g_full"), 1)
                elif k == "VT":
                    n = step[1]
                    pe.wait_ge(sem("g_done"), c.at("g_done", 0 if n == 3 else -1))
                    pe.wait_ge(sem("t_done"), c.at("t_done", -1))
                    t = T[c.even("t_full")]
                    for m_ in range(3):
                        m = nc.tensor.transpose(t[:, m_ * P:m_ * P + P], vT[n % 2][:, m_ * P:m_ * P + P], ident[:, :])
                    m.then_inc(sem("t_full"), 1)
                elif k == "S":
                    u = step[1]
                    j, r = divmod(u, 8)
                    b, h, qt = r // 4, (r // 2) % 2, r % 2
                    if u == 0:
                        pe.wait_ge(sem("g_done"), c.at("g_done", -1))
                        if number == 4:
                            pe.wait_ge(sem("k_lo"), c.at("k_lo"))
                    if r == 0 and u:
                        pe.wait_ge(sem("g_done"), c.at("g_done", -1))
                    if u >= 2:
                        pe.wait_ge(sem("exp"), c.at("exp", -1))
                    s = S[u % 2]
                    q0 = (b * 2 + qt) * P
                    a = over(QX[j % 2], lambda t: t[:, h, q0:q0 + P])
                    for lo, hi in ((0, 512), (512, KV)):
                        m = mm3(s[:, lo:hi], a, over(KX, lambda t: t[:, b * KV + lo:b * KV + hi]), True, True)
                    m.then_inc(sem("s_full"), 1)
                elif k == "T":
                    u = step[1]
                    ahead = min(1, units_of(number) - 1 - u)
                    pe.wait_ge(sem("p_ready"), c.at("p_ready", -ahead))
                    for half in range(2):
                        pe.wait_ge(sem("t_done"), c.at("t_done", half - 1))
                        t = T[c.even("t_full", half)]
                        for m_ in range(3):
                            kk = (3 * half + m_) * P
                            m = nc.tensor.transpose(t[:, m_ * P:m_ * P + P], prob[u % 2][:, kk:kk + P], ident[:, :])
                        m.then_inc(sem("t_full"), 1)
                elif k == "PV":
                    n = step[1]
                    b = n % 2
                    last = 4 * n + 4 == units_of(number)
                    pe.wait_ge(sem("t_done"), c.at("t_done", 0 if last else -2))
                    pe.wait_ge(sem("g_done"), c.at("g_done", -1))
                    heads_out[0] = c.at("g_done", 1)
                    g = G[c.even("g_full")]
                    for kt in range(KVT):
                        m = mm3(g, over(VX, lambda t: t[:, b * KVT + kt, :]), over(PT[n % 2], lambda t: t[:, kt, :]),
                                kt == 0, kt == KVT - 1)
                    m.then_inc(sem("g_full"), 1)
                elif k == "Wo":
                    tt = step[1]
                    if tt in (0, 2):
                        pe.wait_ge(sem("g_done"), heads_out[0])
                        pe.wait_ge(sem("lo_o"), c.at("lo_o"))
                    pe.wait_ge(sem("g_done"), c.at("g_done", -1))
                    g = G[c.even("g_full")]
                    for h in range(2):
                        m = mm3(g, over(OX, lambda t: t[:, h, tt * P:tt * P + P]),
                                over(w_o, lambda t: t[:, h * D:h * D + D]), h == 0, h == 1)
                    m.then_inc(sem("g_full"), 1)
                elif k == "gate":
                    tt = step[1]
                    if tt == 0:
                        pe.wait_ge(sem("gate_split"), 1)
                        pe.wait_ge(sem("t_done"), c.at("t_done"))
                    pe.wait_ge(sem("g_done"), c.at("g_done", -1))
                    g = G[c.even("g_full")]
                    for kt in range(KT):
                        m = mm3(g[:, 0:EXPERTS], over(H, lambda t: latents(t, kt, tt)), over(gate_w, lambda t: t[:, kt, :]),
                                kt == 0, kt == KT - 1)
                    m.then_inc(sem("g_full"), 1)
                elif k == "E":
                    _, e, tt, per = step
                    if tt == 0:
                        pe.wait_ge(sem("lo_e"), c.at("lo_e", e + 1 - min(e + 2, EXPERTS)))
                    pe.wait_ge(sem("g_done"), c.at("g_done", -1))
                    g = G[c.even("g_full")]
                    for kt in range(KT):
                        m = mm3(g, over(H, lambda t: latents(t, kt, tt)), over(ex_w[e % 2], lambda t: t[:, kt * D:kt * D + D]),
                                kt == 0, kt == KT - 1)
                    m.then_inc(sem("g_full"), 1)
                elif k == "TW":
                    which, i = step[1], step[2]
                    pe.wait_ge(sem("t_done"), c.at("t_done", -1))
                    t = T[c.even("t_full")]
                    if which == 0:
                        pe.wait_ge(sem("dq"), c.at("dq"))
                    if which == 2:
                        pe.wait_ge(sem("cut"), c.at("cut"))
                    for m_ in range(4):
                        src = w13_nat[:, 4 * which + m_, :, :].rearrange("p a g -> p (a g)") if which < 2 else w2_cut[:, m_, :]
                        m = nc.tensor.transpose(t[:, m_ * P:m_ * P + P], src, ident[:, :])
                    m.then_inc(sem("t_full"), 1)
                elif k in ("cq", "ck"):
                    b, dt = (0, step[1]) if k == "cq" else step[1:]
                    which = 0 if k == "cq" else 1
                    if k == "cq" and dt == 0:
                        pe.wait_ge(sem("t_done"), c.at("t_done"))
                    pe.wait_ge(sem("x_lo"), which + 1)
                    pe.wait_ge(sem("g_done"), c.at("g_done", -1))
                    g = G[c.even("g_full")]
                    for kt in range(KT):
                        m = mm3(g, over(x_w[which], lambda t: t[:, kt * D + dt * P:kt * D + dt * P + P]),
                                over(H, lambda t: all_latents(t, kt) if k == "cq" else t[:, kt, b, 0:SC]),
                                kt == 0, kt == KT - 1)
                    m.then_inc(sem("g_full"), 1)
                elif k == "cs":
                    tt = step[1]
                    if tt == 0:
                        pe.wait_ge(sem("g_done"), c.at("g_done"))
                    if tt >= 2:
                        pe.wait_ge(sem("c_exp"), tt - 1)
                    for dt in range(KT):
                        m = mm3(Y[tt % 2], over(QC, lambda t: t[:, dt, tt * P:tt * P + P]),
                                over(KC, lambda t: t[:, dt, (tt // 2) * SC:(tt // 2) * SC + SC]), dt == 0, dt == KT - 1)
                    m.then_inc(sem("c_full"), 1)
                elif k == "ct":
                    tt = step[1]
                    pe.wait_ge(sem("c_exp"), tt + 1)
                    pe.wait_ge(sem("t_done"), c.at("t_done", -1))
                    t = T[c.even("t_full")]
                    for m_ in range(4):
                        m = nc.tensor.transpose(t[:, m_ * P:m_ * P + P], prob_c[tt % 2][:, m_ * P:m_ * P + P], ident[:, :])
                    m.then_inc(sem("t_full"), 1)
                elif k == "cpv":
                    tt = step[1]
                    pe.wait_ge(sem("t_done"), c.at("t_done"))
                    if tt == 0:
                        pe.wait_ge(sem("x_lo"), 3)
                    pe.wait_ge(sem("g_done"), c.at("g_done", -1))
                    g = G[c.even("g_full")]
                    for kt in range(4):
                        m = mm3(g, over(PC[tt % 2], lambda t: t[:, kt, :]),
                                over(c_w, lambda t: t[:, (tt // 2) * 4 + kt, :]), kt == 0, kt == 3)
                    m.then_inc(sem("g_full"), 1)
                elif k == "rl":
                    tt = step[1]
                    if tt == 0:
                        pe.wait_ge(sem("t_done"), c.at("t_done"))
                        pe.wait_ge(sem("r_lo"), 1)
                    pe.wait_ge(sem("g_done"), c.at("g_done", -1))
                    g = G[c.even("g_full")]
                    for kt in range(KT):
                        m = mm3(g[:, 0:ROUTED], over(H, lambda t: latents(t, kt, tt)), over(r_w, lambda t: t[:, kt, :]),
                                kt == 0, kt == KT - 1)
                    m.then_inc(sem("g_full"), 1)
                elif k == "rt":
                    tt = step[1]
                    pe.wait_ge(sem("r_dense"), 1)
                    pe.wait_ge(sem("t_done"), c.at("t_done", -1))
                    t = T[c.even("t_full")]
                    nc.tensor.transpose(t[0:ROUTED, 0:P], r_dense[:, tt, :], ident[:, :]).then_inc(sem("t_full"), 1)
                elif k == "rm":
                    tt = step[1]
                    pe.wait_ge(sem("t_done"), c.at("t_done"))
                    pe.wait_ge(sem("r_lo"), 2)
                    pe.wait_ge(sem("g_done"), c.at("g_done", -1))
                    g = G[c.even("g_full")]
                    mm3(g, over(r_T[tt % 2], lambda t: t[:, :]), over(eb_w, lambda t: t[:, :]), True, True)\
                        .then_inc(sem("g_full"), 1)

            walk(c, pe, do)

        @block.scalar
        def _(act):
            c = Counts()
            copy = nc.scalar.activation

            def do(step, number, turn):
                k = step[0]
                if k == "start":
                    act.wait_ge(sem("dma_ctxT"), 16)
                    for kt in range(KT):
                        copy(H[0][:, kt, :, 0:SC], ctxT_raw[:, kt, :, :], ACT.Copy).then_inc(sem("ctx_hi"), 1)
                elif k == "stats":
                    if number in (1, 5):
                        nc.scalar.preload_act_table(ACT.Silu)
                    elif number in (2, 3, 6):
                        nc.scalar.preload_act_table(ACT.Exp)
                    elif number == 4:
                        nc.scalar.preload_act_table_set("natural_log_exp_and_others")
                elif k == "W":
                    slot, dma = step[1], step[2]
                    raw, w = slots[slot][:2]
                    ring = RINGS[slot]
                    users = "d_full" if ring == "dn" else "g_full"
                    if c.any(users):
                        act.wait_ge(sem(users), c.at(users))
                    act.wait_ge(sem(dma), c.at(dma, 16))
                    copy(w[0][:, :], raw[:, :], ACT.Copy).then_inc(sem("hi_" + ring), 1)
                elif k == "xnT":
                    tt = step[1]
                    act.wait_ge(sem("t_full"), c.at("t_full", 1))
                    src = T[c.even("t_full")].rearrange("p (k n) -> p k n", k=KT)
                    copy(latents_all(H[0], tt), src, ACT.Copy).then_inc(sem("hi"), 1)
                elif k == "GU":
                    i = step[1]
                    gated, silu, inner = (gated0, silu0, inner0) if number == 1 else (gated2, silu2, inner2)
                    act.wait_ge(sem("g_full"), c.at("g_full", 1))
                    copy(silu[:, :], G[0], ACT.Silu, scale=sc("gate") if number == 1 else 1.0).then_inc(sem("silu"), 1)
                    act.wait_ge(sem("g_done"), c.at("g_done", 2))
                    copy(inner[i % 2][0][:, :], gated[:, :], ACT.Copy).then_inc(sem("hi"), 1)
                elif k == "K":
                    n, rms = step[1:]
                    act.wait_ge(sem("g_full"), c.at("g_full", 1))
                    g = G[c.even("g_full")][:, 0:384]
                    if rms:
                        copy(k_sq[n % 2], g, ACT.Square).then_inc(sem("k_sq"), 1)
                    else:
                        copy(KX[0][:, 384 * n:384 * n + 384], g, ACT.Copy).then_inc(sem("hi"), 1)
                elif k == "KN":
                    n = step[1]
                    act.wait_ge(sem("g_done"), c.at("g_done", 1))
                    copy(k_r[n % 2][:, :], k_r[n % 2][:, :], ACT.Ln).then_inc(sem("k_ln"), 1)
                    act.wait_ge(sem("k_ln"), c.at("k_ln", 1))
                    copy(k_r[n % 2][:, :], k_r[n % 2][:, :], ACT.Exp, scale=-0.5).then_inc(sem("k_r"), 1)
                elif k == "KM":
                    n = step[1]
                    act.wait_ge(sem("k_raw"), c.at("k_raw", 1))
                    copy(KX[0][:, 384 * n:384 * n + 384], k_raw[n][:, :], ACT.Copy).then_inc(sem("hi"), 1)
                elif k == "q":
                    _, j, h, rms = step
                    act.wait_ge(sem("g_full"), c.at("g_full", 1))
                    g = G[c.even("g_full")]
                    if rms:
                        copy(q_sq[h][:, :], g, ACT.Square).then_inc(sem("q_sq"), 1)
                    copy(QX[j % 2][0][:, h, :], g, ACT.Copy, scale=HD ** -0.5).then_inc(sem("hi"), 1)
                elif k == "VT":
                    n = step[1]
                    act.wait_ge(sem("t_full"), c.at("t_full", 1))
                    copy(VX[0][:, 3 * n:3 * n + 3, :].rearrange("p k n -> p (k n)"), T[c.even("t_full")][:, 0:384],
                         ACT.Copy).then_inc(sem("hi"), 1)
                elif k == "X":
                    u = step[1]
                    j, r = divmod(u, 8)
                    act.wait_ge(sem("bias"), c.at("bias"))
                    col = (r // 2 % 2) * 4 + (r // 4) * 2 + r % 2
                    scale = rq[j % 2][:, col:col + 1] if number == 4 else 1.0
                    copy(prob[u % 2][:, :], S[u % 2], ACT.Exp, bias=nbias[:, u % 4:u % 4 + 1], scale=scale,
                         accum_out=rsum[:, u % 4:u % 4 + 1]).then_inc(sem("exp"), 1)
                elif k == "T":
                    u = step[1]
                    for half in range(2):
                        act.wait_ge(sem("t_full"), c.at("t_full", half + 1))
                        src = T[c.even("t_full", half)][:, 0:384].rearrange("p (k n) -> p k n", k=3)
                        copy(PT[u // 4 % 2][0][:, 3 * half:3 * half + 3, (u % 4) * P:(u % 4) * P + P], src,
                             ACT.Copy).then_inc(sem("hi"), 1)
                elif k == "PV":
                    b = step[1] % 2
                    act.wait_ge(sem("g_full"), c.at("g_full", 1))
                    copy(OX[0][:, :, b * SQ:b * SQ + SQ], G[c.even("g_full")].rearrange("p (h n) -> p h n", h=2),
                         ACT.Copy).then_inc(sem("hi"), 1)
                elif k == "TW":
                    which, i = step[1], step[2]
                    act.wait_ge(sem("t_full"), c.at("t_full", 1))
                    dst, src = turned_weights(which, i, 0, T[c.even("t_full")])
                    copy(dst, src, ACT.Copy).then_inc(sem("hi"), 1)
                elif k == "gate" and step[1] == TT - 1:
                    act.wait_ge(sem("e_bias"), 1)
                    for tt in range(TT):
                        copy(e_exp[:, tt, :], padded[:, tt, 6:WIDE], ACT.Exp, bias=ntop[:, tt:tt + 1])\
                            .then_inc(sem("e_exp"), 1)
                elif k in ("cq", "ck"):
                    if step == ("cq", 0):
                        for which in range(2):
                            act.wait_ge(sem(("dma_xq", "dma_xk")[which]), 16)
                            copy(x_w[which][0][:, :], x_raw[which][:, :], ACT.Copy).then_inc(sem("x_hi"), 1)
                        act.wait_ge(sem("dma_bc"), 16)
                    if step == ("ck", 1, 0):
                        act.wait_ge(sem("dma_c"), 16)
                        copy(c_w[0][:, :, :], c_raw[:, :, :], ACT.Copy).then_inc(sem("x_hi"), 1)
                    act.wait_ge(sem("g_full"), c.at("g_full", 1))
                    dst, bias = crossed(step, 0)
                    copy(dst, G[c.even("g_full")], ACT.Identity, bias=bias).then_inc(sem("hi"), 1)
                elif k == "cs":
                    tt = step[1]
                    act.wait_ge(sem("c_bias"), tt + 1)
                    copy(prob_c[tt % 2][:, :], Y[tt % 2], ACT.Exp, bias=stat_c[:, 1, tt:tt + 1], scale=D ** -0.5,
                         accum_out=stat_c[:, 2, tt:tt + 1]).then_inc(sem("c_exp"), 1)
                elif k == "ct":
                    act.wait_ge(sem("t_full"), c.at("t_full", 1))
                    copy(PC[step[1] % 2][0][:, :, :].rearrange("p k n -> p (k n)"), T[c.even("t_full")], ACT.Copy)\
                        .then_inc(sem("hi"), 1)
                elif k == "rl" and step[1] == TT - 1:
                    act.wait_ge(sem("r_bias"), 1)
                    for tt in range(TT):
                        copy(r_exp[:, tt, :], r_log[:, tt, :], ACT.Exp, bias=r_stat[:, 1, tt:tt + 1],
                             accum_out=r_stat[:, 2, tt:tt + 1]).then_inc(sem("r_exp"), 1)
                elif k == "rt":
                    act.wait_ge(sem("t_full"), c.at("t_full", 1))
                    copy(r_T[step[1] % 2][0][:, :], T[c.even("t_full")][0:ROUTED, 0:P], ACT.Copy).then_inc(sem("hi"), 1)

            walk(c, act, do)

        @block.vector
        def _(dve):
            c = Counts()
            chained = [0]

            def chain(ins):
                chained[0] += 1
                ins.then_inc(sem("dve"), 1)
                dve.wait_ge(sem("dve"), chained[0])

            ts, tt_, stt = nc.vector.tensor_scalar, nc.vector.tensor_tensor, nc.vector.scalar_tensor_tensor

            def split_lo(dst, src, hi_, done, name="hi", more=1):
                dve.wait_ge(sem(name), c.at(name, more))
                tt_(dst, src, f32(hi_), ALU.subtract).then_inc(sem(done), 1)

            def quantise(dst, src, inverse, zero, last):
                chain(ts(src, src, inverse, zero, ALU.mult, ALU.add))
                chain(ts(src, src, ROUND, ROUND + MID, ALU.add, ALU.subtract))
                last(ts(dst, src, -MID, 255.0 - MID, ALU.max, ALU.min))

            def unpack(raw, scales, nib0, nib1, out0, out1, done0, done1, n):
                ts(nib0, raw, 4, None, ALU.arith_shift_right)
                done0(ts(nib1, raw, 28, 28, ALU.logical_shift_left, ALU.arith_shift_right))
                tt_(out0, nib0, scales[:, :, 0:1].to_broadcast([P, n, GROUP]), ALU.mult)
                done1(tt_(out1, nib1, scales[:, :, 1:2].to_broadcast([P, n, GROUP]), ALU.mult))

            def do(step, number, turn):
                k = step[0]
                if k == "start":
                    dve.sem_inc(sem("g_done"), 2)
                    dve.sem_inc(sem("t_done"), 2)
                    dve.wait_ge(sem("dma_small"), 16)
                    d = derived
                    nc.vector.reciprocal(d[:, 0:1], sc("s1"))
                    nc.vector.reciprocal(d[:, 1:2], sc("s2"))
                    ts(d[:, 2:3], sc("z1"), -1.0, MID, ALU.mult, ALU.add)
                    ts(d[:, 3:4], sc("z2"), -1.0, MID, ALU.mult, ALU.add)
                    chain(tt_(d[:, 4:5], sc("s1"), sc("s2"), ALU.mult))
                    chain(stt(d[:, 5:6], d[:, 2:3], float(SC), d[:, 3:4], ALU.mult, ALU.mult))
                elif k == "stats":
                    if number == 0:
                        dve.wait_ge(sem("dma_x"), 16)
                    dve.wait_ge(sem("g_done"), c.at("g_done"))
                    for tt in range(TT):
                        ins_ = nc.vector.bn_stats(moments[:, tt, :], X[:, tt, :])
                    chain(ins_)
                    for tt in range(TT):
                        ins_ = nc.vector.bn_aggr(mean_var[:, tt, :], moments[:, tt, :])
                    chain(ins_)
                    ts(var[:, :], mean_var[:, :, 1], 1e-5, None, ALU.add).then_inc(sem("var"), 1)
                    if number == 0:
                        dve.wait_ge(sem("dma_ctx"), 16)
                        for b in range(B):
                            rows = slice(4 * b, 4 * b + 4)
                            quantise(ctx_q[:, rows, :], ctx_raw[:, rows, :], derived[:, 1:2], sc("z2"),
                                     (lambda i_: i_.then_inc(sem("cq"), 1)) if b else chain)
                    dve.wait_ge(sem("rstd"), number + 1)
                    for tt in range(TT):
                        n_ = ts(xn[:, tt, :], X[:, tt, :], mean_var[:, tt, 0:1], rstd[:, tt:tt + 1], ALU.subtract, ALU.mult)
                        if number:
                            n_.then_inc(sem("xn"), 1)
                        else:
                            chain(n_)
                            quantise(xn[:, tt, :], xn[:, tt, :], derived[:, 0:1], sc("z1"), lambda i_: i_.then_inc(sem("xn"), 1))
                    if number == 4:
                        dve.wait_ge(sem("dma_qk"), 16)
                        chain(tt_(qk_w[:, 2:3], qk_w[:, 0:1], qk_w[:, 1:2], ALU.mult))
                    if number == 3:
                        chain(nc.vector.memset(padded[:, :, 0:6], BIG))
                    if number == 5:
                        chain(nc.vector.memset(w2_nat[:, 4 * INTER:], 0.0))
                elif k == "xqT":
                    tt = step[1]
                    dve.wait_ge(sem("t_full"), c.at("t_full", 1))
                    nc.vector.tensor_copy(xq_T[:, :, tt * P:tt * P + P],
                                          T[c.even("t_full")].rearrange("p (k n) -> p k n", k=KT)).then_inc(sem("t_done"), 1)
                elif k == "xnT":
                    tt = step[1]
                    split_lo(latents_all(H[1], tt), T[c.even("t_full")].rearrange("p (k n) -> p k n", k=KT),
                             latents_all(H[0], tt), "t_done")
                elif k == "sums":
                    dve.wait_ge(sem("csum"), 1)
                    for b in range(B):
                        i_ = ts(cz[:, b, :], Y[b], derived[:, 2:3], None, ALU.mult)
                    dve.wait_ge(sem("rowsum"), 1)
                    chain(ts(row_bias[:, :], Y[2][:, 0:2 * TT:2], derived[:, 3:4], derived[:, 5:6], ALU.mult, ALU.add))
                elif k == "qmm":
                    tt = step[1]
                    dve.wait_ge(sem("g_full"), c.at("g_full", 1))
                    stt(q_tmp[:, :], G[c.even("g_full")], row_bias[:, tt:tt + 1], cz[:, tt // 2, :], ALU.add, ALU.add)\
                        .then_inc(sem("g_done"), 1)
                    dve.wait_ge(sem("g_done"), c.at("g_done", 1))
                    chain(stt(X[:, tt, :], q_tmp[:, :], derived[:, 4:5], X[:, tt, :], ALU.mult, ALU.add))
                elif k == "GU":
                    gated, silu = (gated0, silu0) if number == 1 else (gated2, silu2)
                    if c.any("inner"):
                        dve.wait_ge(sem("inner"), c.at("inner"))
                    dve.wait_ge(sem("silu"), c.at("silu", 1))
                    dve.wait_ge(sem("g_full"), c.at("g_full", 2))
                    stt(gated[:, :], G[1], sc("up") if number == 1 else 1.0, silu[:, :], ALU.mult, ALU.mult)\
                        .then_inc(sem("g_done"), 2)
                elif k == "Yadd":
                    dve.wait_ge(sem("d_full"), c.at("d_full"))
                    for tt in range(TT):
                        i_ = stt(X[:, tt, :], Y[tt], sc("down") if number == 1 else 1.0, X[:, tt, :], ALU.mult, ALU.add)
                    chain(i_)
                elif k == "K":
                    n, rms = step[1:]
                    g = G[c.even("g_full")][:, 0:384]
                    cols = slice(384 * n, 384 * n + 384)
                    if rms:
                        dve.wait_ge(sem("k_sq"), c.at("k_sq", 1))
                        ts(k_raw[n][:, :], g, qk_w[:, 2:3], None, ALU.mult).then_inc(sem("g_done"), 1)
                    else:
                        split_lo(KX[1][:, cols], g, KX[0][:, cols], "g_done")
                elif k == "KN":
                    n = step[1]
                    dve.wait_ge(sem("g_full"), c.at("g_full", 1))
                    ts(k_r[n % 2][:, :], G[c.even("g_full")][:, 0:384], 1.0 / HD, 1e-6, ALU.mult, ALU.add)\
                        .then_inc(sem("g_done"), 1)
                elif k == "KM":
                    n = step[1]
                    dve.wait_ge(sem("k_r"), c.at("k_r"))
                    tt_(k_raw[n][:, :], k_raw[n][:, :], k_r[n % 2][:, :], ALU.mult).then_inc(sem("k_raw"), 1)
                elif k == "q":
                    _, j, h, rms = step
                    dve.wait_ge(sem("hi"), c.at("hi", 1))
                    stt(QX[j % 2][1][:, h, :], G[c.even("g_full")], HD ** -0.5, f32(QX[j % 2][0][:, h, :]), ALU.mult,
                        ALU.subtract).then_inc(sem("g_done"), 1)
                elif k == "QN":
                    dve.wait_ge(sem("g_full"), c.at("g_full", 1))
                    ts(qvar[:, :], G[c.even("g_full")][:, 0:8], 1.0 / HD, 1e-6, ALU.mult, ALU.add).then_inc(sem("g_done"), 1)
                elif k == "V":
                    n = step[1]
                    if number == 4 and n < 2:
                        dve.wait_ge(sem("k_lo"), c.at("k_lo", n - 3))
                    dve.wait_ge(sem("g_full"), c.at("g_full", 1))
                    nc.vector.tensor_copy(vT[n % 2][:, :], G[c.even("g_full")][:, 0:384]).then_inc(sem("g_done"), 1)
                elif k == "VT":
                    n = step[1]
                    flat_v = [v[:, 3 * n:3 * n + 3, :].rearrange("p k n -> p (k n)") for v in VX]
                    split_lo(flat_v[1], T[c.even("t_full")][:, 0:384], flat_v[0], "t_done")
                elif k == "S":
                    u = step[1]
                    j, r = divmod(u, 8)
                    col = (r // 2 % 2) * 4 + (r // 4) * 2 + r % 2
                    dve.wait_ge(sem("s_full"), c.at("s_full", 1))
                    nc.vector.reduce_max(top[:, u % 4:u % 4 + 1], S[u % 2], AX.X).then_inc(sem("s_max"), 1)
                    dve.wait_ge(sem("s_max"), c.at("s_max", 1))
                    if number == 4 and r == 0:
                        dve.wait_ge(sem("rq"), c.at("rq"))
                    scale = rq[j % 2][:, col:col + 1] if number == 4 else 1.0
                    ts(nbias[:, u % 4:u % 4 + 1], top[:, u % 4:u % 4 + 1], scale, -1.0, ALU.mult, ALU.mult)\
                        .then_inc(sem("bias"), 1)
                elif k == "R":
                    u = step[1]
                    dve.wait_ge(sem("exp"), c.at("exp"))
                    nc.vector.reciprocal(rinv[:, u % 4:u % 4 + 1], rsum[:, u % 4:u % 4 + 1]).then_inc(sem("rinv"), 1)
                elif k == "T":
                    u = step[1]
                    for half in range(2):
                        src = T[c.even("t_full", half)][:, 0:384].rearrange("p (k n) -> p k n", k=3)
                        hi_, lo_ = (t[:, 3 * half:3 * half + 3, (u % 4) * P:(u % 4) * P + P] for t in PT[u // 4 % 2])
                        split_lo(lo_, src, hi_, "t_done", more=half + 1)
                elif k == "PV":
                    b = step[1] % 2
                    hi_, lo_ = (t[:, :, b * SQ:b * SQ + SQ] for t in OX)
                    split_lo(lo_, G[c.even("g_full")].rearrange("p (h n) -> p h n", h=2), hi_, "g_done")
                elif k == "Wo":
                    tt = step[1]
                    dve.wait_ge(sem("g_full"), c.at("g_full", 1))
                    dve.wait_ge(sem("g_done"), c.at("g_done"))
                    tt_(X[:, tt, :], G[c.even("g_full")], X[:, tt, :], ALU.add).then_inc(sem("g_done"), 1)
                elif k == "gate":
                    tt = step[1]
                    dve.wait_ge(sem("g_full"), c.at("g_full", 1))
                    nc.vector.tensor_copy(padded[:, tt, 6:WIDE], G[c.even("g_full")][:, 0:EXPERTS]).then_inc(sem("g_done"), 1)
                    if tt == TT - 1:
                        dve.wait_ge(sem("g_done"), c.at("g_done", 1))
                        for t in range(TT):
                            i_ = nc.vector.max(top8[:, t, :], padded[:, t, :])
                        chain(i_)
                        ts(ntop[:, :], top8[:, :, 6], -1.0, None, ALU.mult).then_inc(sem("e_bias"), 1)
                        for t in range(TT):
                            i_ = nc.vector.match_replace(left[:, t, :], top8[:, t, :], padded[:, t, :], -BIG)
                        chain(i_)
                        dve.wait_ge(sem("e_exp"), TT)
                        ts(chosen[:, :, :], left[:, :, 6:WIDE], -BIG, None, ALU.is_le).then_inc(sem("dve"), 1)
                        chained[0] += 1
                        dve.wait_ge(sem("dve"), chained[0])
                        chain(tt_(e_exp[:, :, :], e_exp[:, :, :], chosen[:, :, :], ALU.mult))
                        chain(nc.vector.reduce_sum(e_sum[:, :], e_exp[:, :, :], AX.X))
                        chain(nc.vector.reciprocal(e_inv[:, :], e_sum[:, :]))
                        for t in range(TT):
                            i_ = ts(e_w[:, t, :], e_exp[:, t, :], e_inv[:, t:t + 1], None, ALU.mult)
                        chain(i_)
                elif k == "E":
                    _, e, tt, per = step
                    dve.wait_ge(sem("g_full"), c.at("g_full", 1))
                    dve.wait_ge(sem("g_done"), c.at("g_done"))
                    at = e if turn is None else turn * per + e
                    stt(X[:, tt, :], G[c.even("g_full")], e_w[:, tt, bass.ds(at, 1)], X[:, tt, :], ALU.mult, ALU.add)\
                        .then_inc(sem("g_done"), 1)
                elif k == "DQ2":
                    dve.wait_ge(sem("dma_w2"), 32)
                    nat = w2_nat[:, 0:4 * INTER].rearrange("p (r a g) -> p r a g", a=2, g=GROUP)
                    for nibble, shifts in ((0, (4, None, ALU.arith_shift_right)),
                                           (1, (28, 28, ALU.logical_shift_left, ALU.arith_shift_right))):
                        chain(ts(w2_nib[:, :, :], w2_raw[:, :, :], *shifts))
                        chain(tt_(nat[:, :, nibble, :], w2_nib[:, :, :],
                                  w2_s[:, :, nibble:nibble + 1].to_broadcast([P, 43, GROUP]), ALU.mult))
                elif k == "DQ":
                    i = step[1]
                    dve.wait_ge(sem("t_full"), c.at("t_full"))
                    dma = f"dma_w13_{i % 2}"
                    dve.wait_ge(sem(dma), c.at(dma, 32))
                    raw = w13_raw[i % 2][:, :, :]
                    ts(w13_nib[0][:, :, :], raw, 4, None, ALU.arith_shift_right)
                    ts(w13_nib[1][:, :, :], raw, 28, 28, ALU.logical_shift_left, ALU.arith_shift_right).then_inc(sem("nib"), 1)
                    dve.wait_ge(sem("nib"), c.at("nib", 1))
                    for nibble in range(2):
                        i_ = tt_(w13_nat[:, :, nibble, :], w13_nib[nibble][:, :, :],
                                 w13_s[i % 2][:, :, nibble:nibble + 1].to_broadcast([P, 2 * KT, GROUP]), ALU.mult)
                    i_.then_inc(sem("dq"), 1)
                elif k == "cut":
                    _, i, per = step
                    dve.wait_ge(sem("t_full"), c.at("t_full"))
                    at = i if turn is None else turn * per + i
                    for r in range(4):
                        i_ = nc.vector.tensor_copy(w2_cut[:, r, :], w2_nat[:, bass.ds(at * P + r * INTER, P)])
                    i_.then_inc(sem("cut"), 1)
                elif k == "TW":
                    _, which, i, per = step
                    hi_, src = turned_weights(which, i, 0, T[c.even("t_full")])
                    lo_, _ = turned_weights(which, i, 1, T[c.even("t_full")])
                    split_lo(lo_, src, hi_, "t_done")
                elif k in ("cq", "ck"):
                    dve.wait_ge(sem("hi"), c.at("hi", 1))
                    hi_, bias = crossed(step, 0)
                    lo_, _ = crossed(step, 1)
                    stt(lo_, G[c.even("g_full")], bias, f32(hi_), ALU.add, ALU.subtract).then_inc(sem("g_done"), 1)
                elif k == "cs":
                    tt = step[1]
                    dve.wait_ge(sem("c_full"), tt + 1)
                    chain(nc.vector.reduce_max(stat_c[:, 0, tt:tt + 1], Y[tt % 2], AX.X))
                    ts(stat_c[:, 1, tt:tt + 1], stat_c[:, 0, tt:tt + 1], -D ** -0.5, None, ALU.mult).then_inc(sem("c_bias"), 1)
                elif k == "ct":
                    hi_, lo_ = (t[:, :, :].rearrange("p k n -> p (k n)") for t in PC[step[1] % 2])
                    split_lo(lo_, T[c.even("t_full")], hi_, "t_done")
                elif k == "cpv":
                    tt = step[1]
                    dve.wait_ge(sem("c_exp"), tt + 1)
                    chain(nc.vector.reciprocal(stat_c[:, 3, tt:tt + 1], stat_c[:, 2, tt:tt + 1]))
                    dve.wait_ge(sem("g_full"), c.at("g_full", 1))
                    stt(X[:, tt, :], G[c.even("g_full")], stat_c[:, 3, tt:tt + 1], X[:, tt, :], ALU.mult, ALU.add)\
                        .then_inc(sem("g_done"), 1)
                elif k == "rl":
                    tt = step[1]
                    if tt == 0:
                        dve.wait_ge(sem("dma_rb"), 16)
                    dve.wait_ge(sem("g_full"), c.at("g_full", 1))
                    tt_(r_log[:, tt, :], G[c.even("g_full")][:, 0:ROUTED], r_bias[:, :], ALU.add).then_inc(sem("g_done"), 1)
                    if tt == TT - 1:
                        dve.wait_ge(sem("g_done"), c.at("g_done", 1))
                        chain(nc.vector.reduce_max(r_stat[:, 0, :], r_log[:, :, :], AX.X))
                        ts(r_stat[:, 1, :], r_stat[:, 0, :], -1.0, None, ALU.mult).then_inc(sem("r_bias"), 1)
                        dve.wait_ge(sem("r_exp"), TT)
                        chain(nc.vector.reciprocal(r_stat[:, 3, :], r_stat[:, 2, :]))
                        for t in range(TT):
                            i_ = ts(r_sc[:, t, :], r_exp[:, t, :], r_stat[:, 3, t:t + 1], None, ALU.mult)
                        chain(i_)
                        for t in range(TT):
                            i_ = nc.vector.max(r_top[:, t, :], r_sc[:, t, :])
                        chain(i_)
                        for t in range(TT):
                            i_ = nc.vector.match_replace(r_left[:, t, :], r_top[:, t, :], r_sc[:, t, :], -1.0)
                        chain(i_)
                        stt(r_dense[:, :, :], r_left[:, :, :], 0.0, r_sc[:, :, :], ALU.is_lt, ALU.mult).then_inc(sem("r_dense"), 1)
                        chain(nc.vector.reduce_sum(r_stat[:, 4, :], r_top[:, :, :], AX.X))
                        for t in range(TT):
                            i_ = stt(X[:, t, :], xn[:, t, :], r_stat[:, 4, t:t + 1], X[:, t, :], ALU.mult, ALU.add)
                        chain(i_)
                elif k == "rt":
                    hi_, lo_ = (t[:, :] for t in r_T[step[1] % 2])
                    split_lo(lo_, T[c.even("t_full")][0:ROUTED, 0:P], hi_, "t_done")
                elif k == "rm":
                    tt = step[1]
                    dve.wait_ge(sem("g_full"), c.at("g_full", 1))
                    tt_(X[:, tt, :], G[c.even("g_full")], X[:, tt, :], ALU.add).then_inc(sem("g_done"), 1)

            walk(c, dve, do)
            dve.wait_ge(sem("g_done"), c.at("g_done"))
            nc.vector.memset(var[:, 0:1], 0.0).then_inc(sem("result"), 1)

        @block.gpsimd
        def _(pool):
            c = Counts()

            def hi_part(dst, src):
                return nc.gpsimd.tensor_scalar(dst, src, 1.0, 1.0, ALU.mult, ALU.mult)

            def lo_part(dst, src, hi_):
                return nc.gpsimd.tensor_tensor(dst, src, f32(hi_), ALU.subtract)

            def split(w, raw, own, done):
                hi_part(w[0], raw).then_inc(sem(own), 1)
                split_count[0] += 1
                pool.wait_ge(sem(own), split_count[0])
                lo_part(w[1], raw, w[0]).then_inc(sem(done), 1)

            split_count = [0]

            def do(step, number, turn):
                k = step[0]
                if k == "start":
                    nc.gpsimd.memset(neg_half[:, :], -0.5)
                    nc.gpsimd.memset(zeros_bf[:, :], 0.0)
                    nc.gpsimd.memset(ones_bf[:, :], 1.0)
                    nc.gpsimd.memset(ones[:, :], 1.0)
                    nc.gpsimd.memset(ident[:, :], 0.0).then_inc(sem("blank"), 1)
                    pool.wait_ge(sem("blank"), 1)
                    nc.gpsimd.affine_select(out=ident[:, :], in_=ident[:, :], compare_op=ALU.not_equal, fill=1.0, base=0,
                                            pattern=[[-1, P]], channel_multiplier=1).then_inc(sem("const"), 1)
                elif k == "stats":
                    pool.wait_ge(sem("var"), number + 1)
                    nc.gpsimd.tensor_tensor(rstd[:, :], var[:, :], neg_half[:, 0:TT], ALU.pow).then_inc(sem("rstd"), 1)
                    if number == 0:
                        for kt in range(KT):
                            pool.wait_ge(sem("ctx_hi"), kt + 1)
                            lo_part(H[1][:, kt, :, 0:SC], ctxT_raw[:, kt, :, :], H[0][:, kt, :, 0:SC]).then_inc(sem("ctx_lo"), 1)
                    if number == 3:
                        pool.wait_ge(sem("dma_gate"), 16)
                        split((gate_w[0][:, :, :], gate_w[1][:, :, :]), gate_raw[:, :, :], "pool", "gate_split")
                    if number == 7:
                        pool.wait_ge(sem("dma_r"), 16)
                        split((r_w[0][:, :, :], r_w[1][:, :, :]), r_raw[:, :, :], "pool", "r_lo")
                        pool.wait_ge(sem("dma_eb"), 16)
                        split((eb_w[0][:, :], eb_w[1][:, :]), eb_raw[:, :], "pool", "r_lo")
                elif k == "W":
                    raw, w = slots[step[1]][:2]
                    ring = RINGS[step[1]]
                    pool.wait_ge(sem("hi_" + ring), c.at("hi_" + ring, 1))
                    lo_part(w[1][:, :], raw[:, :], w[0][:, :]).then_inc(sem("lo_" + ring), 1)
                elif k == "GU":
                    i = step[1]
                    gated, inner = (gated0, inner0) if number == 1 else (gated2, inner2)
                    pool.wait_ge(sem("hi"), c.at("hi", 1))
                    lo_part(inner[i % 2][1][:, :], gated[:, :], inner[i % 2][0][:, :]).then_inc(sem("inner"), 1)
                elif k == "R":
                    u = step[1]
                    pool.wait_ge(sem("rinv"), c.at("rinv", 1))
                    pool.sem_inc(sem("p_begun"), 1)
                    nc.gpsimd.tensor_scalar(prob[u % 2][:, :], prob[u % 2][:, :], rinv[:, u % 4:u % 4 + 1], 1.0,
                                            ALU.mult, ALU.mult).then_inc(sem("p_ready"), 1)
                elif k == "KM":
                    n = step[1]
                    cols = slice(384 * n, 384 * n + 384)
                    pool.wait_ge(sem("hi"), c.at("hi", 1))
                    lo_part(KX[1][:, cols], k_raw[n][:, :], KX[0][:, cols]).then_inc(sem("k_lo"), 1)
                elif k == "QN":
                    j = step[1]
                    pool.wait_ge(sem("g_done"), c.at("g_done", 1))
                    nc.gpsimd.tensor_tensor(rq[j % 2][:, :], qvar[:, :], neg_half[:, :], ALU.pow).then_inc(sem("rq"), 1)
                elif step == ("cq", 0):
                    for n, (w, raw) in enumerate(((x_w[0], x_raw[0][:, :]), (x_w[1], x_raw[1][:, :]), (c_w, c_raw[:, :, :]))):
                        pool.wait_ge(sem("x_hi"), n + 1)
                        whole = (slice(None),) * len(raw.shape)
                        lo_part(w[1][whole], raw, w[0][whole]).then_inc(sem("x_lo"), 1)

            walk(c, pool, do)


def kernel(**inputs):
    import numpy as np
    import concourse.bacc as _bacc
    from concourse import mybir as _mybir
    from concourse.bass_utils import run_bass_kernel_spmd as _run

    v = {k: np.asarray(a) for k, a in inputs.items()}

    def tiled(w):
        return w.reshape(-1, P, w.shape[-1]).transpose(1, 0, 2)

    def attention_chunks(n, heads_kv):
        wq, wk, wv, wo = (v[f"L{n}_xattn_W{x}"] for x in "qkvo")
        pairs = HEADS // heads_kv // 2
        out = []
        for g in range(heads_kv):
            kv_cols = slice(g * HD, g * HD + HD)
            out.append(np.concatenate([tiled(wk[:, kv_cols]), tiled(wv[:, kv_cols])], axis=2).reshape(P, -1))
            for j in range(pairs):
                q_cols = slice((g * pairs + j) * 2 * HD, (g * pairs + j + 1) * 2 * HD)
                out.append(tiled(wq[:, q_cols]).reshape(P, -1))
                out.append(tiled(wo[q_cols, :]).reshape(P, -1))
        return np.stack(out)

    def padded_rows(w, n):
        return np.concatenate([w, np.zeros((n - w.shape[0], *w.shape[1:]), w.dtype)])

    gate_t, up_t = (tiled(padded_rows(v[f"L0_ffn_{x}_w"], IT * P).T) for x in ("gate", "up"))
    down_t = padded_rows(v["L0_ffn_down_w"].T, IT * P)
    ffn0 = [np.concatenate([np.concatenate([g[:, :, i * P:i * P + P] for g in (gate_t, up_t)], axis=2).reshape(P, -1),
                            down_t[i * P:i * P + P]], axis=1) for i in range(IT)]
    packed = [padded_rows(v[f"L2_ffn_w{i}"].reshape(INTER, KT * GROUP), IT * P).reshape(IT, P, KT * GROUP) for i in (1, 3)]
    scales = [padded_rows(v[f"L2_ffn_s{i}"].reshape(INTER, 2 * KT), IT * P).reshape(IT, P, 2 * KT) for i in (1, 3)]
    experts = v["L1_ffn_expert_w"].reshape(EXPERTS, KT, P, D).transpose(0, 2, 1, 3).reshape(EXPERTS, P, KT * D)
    small = [v[f"L0_xattn_{x}"] for x in ("x1_scale", "x1_zp", "x2_scale", "x2_zp")]
    small += [v[f"L0_ffn_{x}_scale"] for x in ("gate", "up", "down")]
    c4 = v["ctx_4096"]
    arrays = {
        "x": v["x"],
        "ctx": c4,
        "ctxT": c4.transpose(2, 0, 1).reshape(KT, P, B, SC).transpose(1, 0, 2, 3),
        "small": np.broadcast_to(np.stack([a.reshape(()) for a in small]), (P, 7)),
        "w_ffn0": np.stack(ffn0),
        "w_attn1": attention_chunks(1, LAYER[1]["kv"]),
        "w_attn2": attention_chunks(2, LAYER[2]["kv"]),
        "qk_norm": np.stack([v["L2_xattn_q_norm_w"], v["L2_xattn_k_norm_w"]], axis=1),
        "gate_w": tiled(v["L1_ffn_gate_w"]),
        "w_experts": experts,
        "w2": v["L2_ffn_w2"].reshape(P, 43, GROUP),
        "s2": v["L2_ffn_s2"].reshape(P, 43, 2),
        "w13": np.concatenate(packed, axis=2),
        "s13": np.concatenate(scales, axis=2),
        "w_cross": np.stack([tiled(v[f"L3_xattn_W{x}"].T).reshape(P, -1) for x in "qk"]),
        "b_cross": np.stack([v[f"L3_xattn_b{x}"].reshape(KT, P).T for x in "qk"], axis=1),
        "router_w": tiled(v["L3_ffn_router_weight"].T),
        "router_b": np.broadcast_to(v["L3_ffn_router_bias"], (P, ROUTED)),
        "expert_b": v["L3_ffn_expert_bias"],
    }
    arrays = {k: np.ascontiguousarray(a) for k, a in arrays.items()}
    nc = _bacc.Bacc("TRN2", target_bir_lowering=False, num_devices=1)
    ins = {k: nc.dram_tensor("in_" + k, a.shape, _mybir.dt.from_np(a.dtype), kind="ExternalInput").ap()
           for k, a in arrays.items()}
    out = nc.dram_tensor("out", (B, SQ, D), F32, kind="ExternalOutput").ap()
    build_program(nc, ins, out)
    r = _run(nc, [{"in_" + k: a for k, a in arrays.items()}], core_ids=[0])
    return r.results[0]["out"]
```

```python
from collections import Counter
from contextlib import ExitStack

import concourse.bass as bass
from concourse import mybir

F32 = mybir.dt.float32
F32R = mybir.dt.float32r
BF16 = mybir.dt.bfloat16
I32 = mybir.dt.int32
ALU = mybir.AluOpType
ACT = mybir.ActivationFunctionType
AX = mybir.AxisListType

P = 128
B, SQ, D = 2, 256, 512
SC = 512
KT = D // P
TT = B * SQ // P
KV = SC + SQ
KVT = KV // P
HD = 128
HEADS = 32
INTER = 1376
IT = -(-INTER // P)
EXPERTS = 8
ROUTED = 64
GROUP = 64
HALF = GROUP // 2
BLOCKS = 8
ROUND = 1.5 * 2.0 ** 23
MID = 128.0
BIG = 3.0e38
NIBBLES = ((4, None, ALU.arith_shift_right), (28, 28, ALU.logical_shift_left, ALU.arith_shift_right))

LAYER = {1: dict(kv=4, pairs=4, rms=False), 2: dict(kv=8, pairs=2, rms=True)}


def adds(step):
    k = step[0]
    if k == "W":
        ring = RINGS[step[1]]
        return {step[2]: 16, "hi_" + ring: 1, "lo_" + ring: 1}
    if k == "H":
        return {step[2]: 16, "hi_" + RINGS[step[1]]: 1}
    if k == "L":
        return {"lo_" + RINGS[step[1]]: 1}
    if k == "K":
        return {"g_full": 1, "g_done": 1, "k_sq" if step[2] else "hi": 1}
    if k == "KN":
        return {"t_full": 1, "t_done": 1, "k_ln": 1, "k_r": 1}
    if k == "KM":
        return {"k_raw": 1, "hi": 1, "k_lo": 1}
    if k == "q":
        return {"g_full": 1, "g_done": 1, "hi": 1, **({"q_sq": 1} if step[3] else {})}
    if k == "QN":
        return {"g_full": 1, "g_done": 1, "rq": 1}
    if k in ("PV", "cq", "ck"):
        return {"g_full": 1, "g_done": 1, "hi": 1}
    if k in ("V", "Wo", "E", "gate", "qmm", "cpv", "rl", "rm"):
        return {"g_full": 1, "g_done": 1}
    if k in ("VT", "xnT", "ct", "rt"):
        return {"t_full": 1, "t_done": 1, "hi": 1}
    if k == "xqT":
        return {"t_full": 1, "t_done": 1}
    if k == "TW":
        return {"t_full": 1, "t_done": 1, "hi": 1}
    if k == "cut":
        return {"cut": 1}
    if k == "S":
        return {"s_full": 1, "s_max": 1, "bias": 1}
    if k == "X":
        return {"exp": 1}
    if k == "R":
        return {"rinv": 1, "p_ready": 1}
    if k == "T":
        return {"t_full": 2, "t_done": 2, "hi": 2}
    if k == "GU":
        return {"g_full": 2, "g_done": 2, "silu": 1, "hi": 1, "inner": 1}
    if k == "D":
        return {"y_full": TT} if step[1] == IT - 1 else {"d_full": 1}
    if k == "split":
        return {"x_hi": 1, "x_lo": 1}
    if k == "bn":
        return {"var": 1, "rstd": 1}
    if k == "xn":
        return {"xn": 1}
    if k == "DQ":
        return {f"dma_w13_{step[1] % 2}": 32, "nib": 1, "dq": 1}
    return {}


RINGS = {"gu0": "gu", "gu1": "gu", "dn0": "dn", "dn1": "dn", "kv": "rq", "q": "rq", "o": "o", "e0": "e", "e1": "e"}


class Counts:

    def __init__(self):
        self.base, self.here = Counter(g_done=2, t_done=2), Counter()
        self.per, self.turn = Counter(), None

    def any(self, sem, more=0):
        return self.base[sem] + self.here[sem] + more > 0

    def at(self, sem, more=0):
        v = self.base[sem] + self.here[sem] + more
        return v if self.turn is None or not self.per[sem] else self.turn * self.per[sem] + v

    def even(self, sem, more=0):
        assert self.turn is None or self.per[sem] % 2 == 0, sem
        return (self.base[sem] + self.here[sem] + more) % 2

    def enter(self, turn, steps):
        self.base.update(self.here)
        self.here, self.turn, self.per = Counter(), turn, Counter()
        for s in steps:
            self.per.update(adds(s))

    def leave(self, turns):
        assert +self.here == +self.per, (self.here, self.per)
        for k, v in self.per.items():
            self.base[k] += v * turns
        self.here, self.turn, self.per = Counter(), None, Counter()


def turned():
    return [("xnT", tt) for tt in range(TT)]


def followed(number, jobs):
    if number == BLOCKS:
        return sum(jobs, [])

    def bn(tt):
        return ("bn", number, tt)

    def xn(tt):
        return ("xn", number, tt)
    return [*jobs[0], bn(0), *jobs[1], bn(1), *jobs[2], bn(2), xn(0), xn(1), *jobs[3], bn(3), xn(2), xn(3)]


def ffn_segments(quantised):
    def w(name, i, per=0):
        slot = f"{name}{i % 2}"
        return [("W", slot, "dma_" + slot, i, per)] if i < IT else []

    def dq(i, per=0):
        return [("DQ", i, per)] if i < IT else []

    def cut(i, per=0):
        return [("cut", i, per)] if i < IT else []

    def tw(which, i, per=0):
        return [("TW", which, i, per)] if i < IT else []

    def body(i, per):
        out = []
        for j in (i, i + 1):
            if quantised:
                out += [("GU", j + 1), *cut(j + 2, per), *tw(0, j + 2, per), *tw(1, j + 2, per), ("D", j),
                        *tw(2, j + 2, per), *dq(j + 3, per)]
            else:
                out += [("GU", j + 1), *w("gu", j + 3, per), ("D", j), *w("dn", j + 2, per)]
        return out

    n = (IT - 1) // 2 - 1
    if quantised:
        t = turned()
        begin = [("begin",), *t[0:2], ("DQ", 1, 0), *t[2:4], ("zeroY",), ("TW", 0, 1, 0), ("TW", 1, 1, 0), ("DQ2", 0), ("GU", 0),
                 ("DQ2", 1), ("GU", 1), ("cut", 0, 0), ("TW", 2, 0, 0), ("DQ", 2, 0),
                 ("D", 0), ("cut", 1, 0), ("TW", 2, 1, 0), ("cut", 2, 0), ("TW", 0, 2, 0), ("TW", 1, 2, 0),
                 ("TW", 2, 2, 0), ("DQ", 3, 0), ("x",)]
        n = (IT - 1) // 2 - 2
        end = [*body(2 * n + 1, 0), *body(2 * n + 3, 0)[:2]]
        then = end.index(("GU", IT - 1))
        end = [*end[:then], ("split", "xk", 1), *end[then:], ("D", IT - 1)]
        return [(1, begin), (n, body(1, 2)), (1, [*end, *followed(6, [[("Yadd", 0)], [("Yadd", 1)], [("ck", 0, 0), ("Yadd", 2)],
                                                                         [("ck", 0, 1), ("Yadd", 3)]])])]
    begin = [*turned(), ("zeroY",), ("GU", 0), *w("gu", 2), *w("dn", 1)]
    end = [*body(2 * n, 0), ("D", IT - 1)]
    for chunk, d in zip(first_chunks(), (IT - 3, IT - 2)):
        at = end.index(("D", d))
        end = [*end[:at], chunk, *end[at:]]
    return [(1, begin), (n, body(0, 2)), (1, [*end, *followed(2, [[("Yadd", tt)] for tt in range(TT)])])]


def first_chunks():
    return [("W", "kv", "dma_rq", 0, 0), ("W", "q", "dma_rq", 1, 0)]


def attention_segments(layer):
    n_kv, pairs, rms = LAYER[layer]["kv"], LAYER[layer]["pairs"], LAYER[layer]["rms"]
    units = 8 * pairs

    def turn(first, per, more):
        def chunk(j, kind):
            return first + (j // pairs) * (1 + 2 * pairs) + kind + 2 * (j % pairs)

        def wkv():
            return [("W", "kv", "dma_rq", first + 1 + 2 * pairs, per)] if more else []

        def wq(j):
            return [("W", "q", "dma_rq", chunk(j, 1), per)] if more or j < pairs else []

        def wo(j):
            return [("W", "o", "dma_ro", chunk(j, 2), per)] if more or j < pairs else []

        def q(j, h):
            return [("q", j, h, rms)] if more or j < pairs else []

        def qn(j):
            return [("QN", j)] if rms and (more or j < pairs) else []

        def k(n):
            return [("K", n, rms)] if more else []

        def kn(n):
            return [("KN", n)] if rms and more else []

        def km(n):
            return [("KM", n)] if rms and more else []

        out = [("V", 0), ("V", 1), ("S", 0), ("VT", 0), ("S", 1), ("X", 0), ("V", 2), ("R", 0), ("X", 1), ("VT", 1), ("R", 1), ("VT", 2)]
        for u in range(units - 2):
            j, r = divmod(u, 8)
            out += [("S", u + 2), ("T", u), ("X", u + 2)]
            wo_at = (1, 2) if more or j < pairs - 1 else (2, 4)
            if r == 0 and j:
                out += [("PV", 2 * j - 1)]
            elif u == 1:
                out += [("V", 3)]
            elif r == 3:
                out += q(j + 1, 0)
                if u == 3:
                    out += [("VT", 3)]
            elif r == 4:
                out += [*q(j + 1, 1), *wq(j + 2)]
            elif r == 5:
                out += [*qn(j + 1), ("PV", 2 * j)]
            elif r > 5:
                out += [("Wo", r - 6), *(wkv() if u == 7 else [])]
            if j and r == wo_at[0]:
                out += [("Wo", 2)]
            if j and r == wo_at[1]:
                out += [("Wo", 3), *wo(j)]
            out += [("R", u + 2)]
        if more:
            return out + [("T", units - 2), *k(0), ("Wo", 0), *k(1), *kn(0), ("T", units - 1), ("Wo", 1), *k(2),
                          *km(0), *kn(1), ("PV", 2 * pairs - 1), *k(3), *km(1), *kn(2), ("Wo", 2), *km(2), *kn(3),
                          ("Wo", 3), *km(3), *wo(pairs)]
        last = 2 * pairs - 1
        if layer == 1:
            return [*out,
                    *followed(3, [[("T", units - 2), ("Wo", 0)], [("T", units - 1), ("Wo", 1)],
                                  [("PV", last), ("H", "e0", "dma_e0", 0, 0), ("Wo", 2)], [("Wo", 3)]]), ("L", "e0")]
        return [*out, *followed(5, [[("T", units - 2), ("Wo", 0)], [("T", units - 1), ("DQ", 0, 0), ("w2load",), ("Wo", 1)],
                                    [("PV", last), ("TW", 0, 0, 0), ("TW", 1, 0, 0), ("Wo", 2)], [("Wo", 3)]])]

    per = 1 + 2 * pairs
    def keys_of(n):
        return [("K", n, rms)], [("KN", n)] if rms else [], [("KM", n)] if rms else []
    (k0, n0, m0), (k1, n1, m1), (k2, n2, m2), (k3, n3, m3) = map(keys_of, range(4))
    t = turned()
    first = [("begin",), *k0, *t[0:2], *k2, *n0, *t[2:4], *n2, *m0, *k1, *m2, *k3, *n1, ("q", 0, 0, rms), *m1, *n3,
             ("q", 0, 1, rms), *m3, ("W", "o", "dma_ro", 2, 0), ("W", "q", "dma_rq", 3, 0), *([("QN", 0)] if rms else [])]
    return [(1, first), (n_kv - 1, turn(0, per, True)), (1, turn((n_kv - 1) * per, 0, False))]


def experts_segments():
    def w(e, per=0):
        return [("W", f"e{e % 2}", f"dma_e{e % 2}", e, per)] if e < EXPERTS else []

    def pair(e, per):
        out = []
        for x in (e, e + 1):
            out += [*[("E", x, tt, per) for tt in range(TT)], *w(x + 2, per)]
        return out
    n = EXPERTS // 2 - 1
    last = EXPERTS - 1
    return [(1, [("begin",), *turned(), *[("gate", tt) for tt in range(TT)], *w(1)]), (n, pair(0, 2)),
            (1, [*[("E", last - 1, tt, 0) for tt in range(TT)], *first_chunks(),
                 *followed(4, [[("E", last, tt, 0)] for tt in range(TT)])])]


def cross_steps():
    keys = [("ck", b, dt) for b in range(B) for dt in range(KT)]
    out = [keys[2], ("begin",), ("split", "xq", 0), *keys[3:6], *turned(), ("c",), *keys[6:], ("router",),
           *[("cq", dt) for dt in range(KT)], ("split", "c", None), ("cs", 0), ("cs", 1)]
    jobs = [[("ct", 0), ("cs", 2), ("ct", 1), ("cpv", 0)], [("cs", 3), ("ct", 2), ("cpv", 1)],
            [("ct", 3), ("cpv", 2)], [("cpv", 3)]]
    return out + followed(7, jobs)


def router_steps():
    return [("begin",), *turned(), ("rl", 0), ("rl", 1), ("top", 0), ("choose", 0), ("rl", 2), ("rx", 0), ("rx", 1), ("rl", 3),
            ("top", 1), ("rt", 0), ("rt", 1), ("choose", 1), ("rm", 0), ("rm", 1), ("rt", 2), ("rt", 3),
            ("rx", 2), ("rx", 3), ("rm", 2), ("rm", 3)]


def segments(blocks):
    start = [("start",), *followed(0, [[]] * TT), ("scale", 0), ("xqT", 0), ("xqT", 1), ("scale", 1), ("xqT", 2), ("xqT", 3),
             ("W", "gu0", "dma_gu0", 0, 0), ("W", "dn0", "dma_dn0", 0, 0), ("W", "gu1", "dma_gu1", 1, 0), ("context",),
             ("quantise", 0), ("quantise", 1), ("sums", 0),
             *followed(1, [[("qmm", 0)], [("sums", 1), ("qmm", 1)], [("qmm", 2)], [("qmm", 3)]]), ("lows",)]
    out = [[(1, start)], ffn_segments(False), attention_segments(1), experts_segments(), attention_segments(2),
           ffn_segments(True), [(1, cross_steps())], [(1, router_steps())]]
    return out[:blocks]


def build_program(nc, ins, out, blocks=8):
    ctx = ExitStack()
    with ctx:
        sems = {}

        def sem(name):
            if name not in sems:
                sems[name] = ctx.enter_context(nc.semaphore(name))
            return sems[name]

        def sb(scope, name, shape, dt=F32):
            return scope.enter_context(nc.sbuf_tensor(name, shape, dt))

        def pair(scope, name, shape):
            return (sb(scope, name + "_hi", shape, F32R), sb(scope, name + "_lo", shape, F32R))

        X = sb(ctx, "X", [P, TT, D])
        H = pair(ctx, "H", [P, KT, B, KV])
        ident = sb(ctx, "ident", [P, P])
        ones = sb(ctx, "ones", [P, P])
        zeros_bf = sb(ctx, "zeros_bf", [P, D], BF16)
        ones_bf = sb(ctx, "ones_bf", [P, P], BF16)
        neg_half = sb(ctx, "neg_half", [P, 8])
        small = sb(ctx, "small", [P, 7])
        moments = sb(ctx, "moments", [P, TT, 6])
        mean_var = sb(ctx, "mean_var", [P, TT, 2])
        var = sb(ctx, "var", [P, TT])
        rstd = sb(ctx, "rstd", [P, TT])
        qk_w = sb(ctx, "qk_w", [P, 3])
        gate_raw = sb(ctx, "gate_raw", [P, KT, EXPERTS])
        gate_w = pair(ctx, "gate_w", [P, KT, EXPERTS])
        HIGH = 118080
        start = nc.sbuf_bytes_remaining

        def fill(scope, name, n):
            gap = n - (start - nc.sbuf_bytes_remaining)
            assert gap >= 0, name
            if gap:
                sb(scope, name, [P, gap // 4])

        with ExitStack() as scope:
            xn = sb(scope, "xn", [P, TT, D])
            ctx_raw = sb(scope, "ctx_raw", [P, B * SC // P, D])
            ctxT_raw = sb(scope, "ctxT_raw", [P, KT, B, SC])
            ctx_q = sb(scope, "ctx_q", [P, B * SC // P, D], BF16)
            xq_T = sb(scope, "xq_T", [P, KT, TT * P], BF16)
            derived = sb(scope, "derived", [P, 8])
            cz = sb(scope, "cz", [P, B, D])
            row_bias = sb(scope, "row_bias", [P, TT])
            q_tmp = sb(scope, "q_tmp", [P, D])
            inner0 = [pair(scope, f"inner0{i}", [P, TT * P]) for i in range(2)]
            gated0 = sb(scope, "gated0", [P, TT * P])
            silu0 = sb(scope, "silu0", [P, TT * P])
            gu_raw = [sb(scope, f"gu_raw{i}", [P, 2 * KT * P]) for i in range(2)]
            dn_raw = [sb(scope, f"dn_raw{i}", [P, D]) for i in range(2)]
            gu0 = [pair(scope, f"gu{i}", [P, 2 * KT * P]) for i in range(2)]
            dn0 = [pair(scope, f"dn{i}", [P, D]) for i in range(2)]

        with ExitStack() as scope:
            PT = [pair(scope, f"PT{i}", [P, KVT, 4 * P]) for i in range(2)]
            KX = pair(scope, "KX", [P, B * KV])
            VX = pair(scope, "VX", [P, B * KVT, HD])
            vT = [sb(scope, f"vT{i}", [P, 3 * P]) for i in range(2)]
            k_raw = [*vT, *[sb(scope, f"k_raw{i}", [P, 3 * P]) for i in range(2)]]
            prob = [sb(scope, f"prob{i}", [P, KV]) for i in range(2)]
            QX = [pair(scope, f"QX{i}", [P, 2, TT * P]) for i in range(2)]
            OX = pair(scope, "OX", [P, 2, TT * P])
            q_sq = [sb(scope, f"q_sq{i}", [P, TT * P]) for i in range(2)]
            k_sq = [t[:, 0:3 * P] for t in q_sq]
            k_r = [sb(scope, f"k_r{i}", [P, 3 * P]) for i in range(2)]
            top = sb(scope, "top", [P, 4])
            nbias = sb(scope, "nbias", [P, 4])
            rsum = sb(scope, "rsum", [P, 4])
            rinv = sb(scope, "rinv", [P, 4])
            qvar = sb(scope, "qvar", [P, 8])
            rq = [sb(scope, f"rq{i}", [P, 8]) for i in range(2)]
            fill(scope, "pad_a", HIGH)
            raw_q = sb(scope, "raw_q", [P, 1024])
            raw_o = sb(scope, "raw_o", [P, 1024])
            w_kv = pair(scope, "w_kv", [P, 1024])
            w_q = pair(scope, "w_q", [P, 1024])
            w_o = pair(scope, "w_o", [P, 1024])
        with ExitStack() as scope:
            sb(scope, "pad1", [P, TT, D])
            WIDE = EXPERTS + 6
            padded = sb(scope, "padded", [P, TT, WIDE])
            top8 = sb(scope, "top8", [P, TT, 8])
            left = sb(scope, "left", [P, TT, WIDE])
            chosen = sb(scope, "chosen", [P, TT, EXPERTS])
            ntop = sb(scope, "ntop", [P, TT])
            e_exp = sb(scope, "e_exp", [P, TT, EXPERTS])
            e_sum = sb(scope, "e_sum", [P, TT])
            e_inv = sb(scope, "e_inv", [P, TT])
            e_w = sb(scope, "e_w", [P, TT, EXPERTS])
            ex_raw1, ex_w1 = sb(scope, "ex_raw1", [P, KT * D]), pair(scope, "ex_w1", [P, KT * D])
            fill(scope, "pad_e", HIGH)
            ex_raw = [sb(scope, "ex_raw0", [P, KT * D]), ex_raw1]
            ex_w = [pair(scope, "ex_w0", [P, KT * D]), ex_w1]

        with ExitStack() as scope:
            sb(scope, "pad2", [P, TT, D])
            inner2 = [pair(scope, f"inner2{i}", [P, TT * P]) for i in range(2)]
            gated2 = sb(scope, "gated2", [P, TT * P])
            silu2 = sb(scope, "silu2", [P, TT * P])
            gu2 = [pair(scope, f"gu2{i}", [P, 2 * KT * P]) for i in range(2)]
            dn2 = [pair(scope, f"dn2{i}", [P, D]) for i in range(2)]
            w2_nat = sb(scope, "w2_nat", [P, 4 * INTER + P], I32)
            w2_half = sb(scope, "w2_half", [P, (4 * INTER + P) // HALF])
            w2_cut = sb(scope, "w2_cut", [P, 4, P])
            fill(scope, "pad_f", HIGH)
            w13_raw = [sb(scope, f"w13_raw{i}", [P, 2 * KT, GROUP], I32) for i in range(2)]
            w13_s = [sb(scope, f"w13_s{i}", [P, 2 * KT, 2]) for i in range(2)]
            w13_nib = [sb(scope, f"w13_nib{i}", [P, 2 * KT, GROUP], I32) for i in range(2)]
            w13_nat = sb(scope, "w13_nat", [P, 2 * KT, 2, GROUP])
            w2_raw = sb(scope, "w2_raw", [P, 43, GROUP], I32)
            w2_s = sb(scope, "w2_s", [P, 43, 2])

        with ExitStack() as scope:
            c_raw = sb(scope, "c_raw", [P, B * SC // P, D])
            QC = pair(scope, "QC", [P, KT, TT * P])
            c_w = pair(scope, "c_w", [P, B * SC // P, D])
            x_w0 = pair(scope, "x_w0", [P, KT * D])
            KC = pair(scope, "KC", [P, KT, B * SC])
            stat_c = sb(scope, "stat_c", [P, 4, TT])
            bias_c = sb(scope, "bias_c", [P, 2, KT])
            fill(scope, "pad_c", HIGH)
            x_w = [x_w0, pair(scope, "x_w1", [P, KT * D])]
            with ExitStack() as inner_scope:
                x_raw1 = sb(inner_scope, "x_raw1", [P, KT * D])
                x_raw = [sb(inner_scope, "x_raw0", [P, KT * D]), x_raw1]
            prob_c = [sb(scope, f"prob_c{i}", [P, SC]) for i in range(2)]
            PC = [pair(scope, f"PC{i}", [P, SC // P, P]) for i in range(2)]
            r_raw = sb(scope, "r_raw", [P, KT, ROUTED])
            r_w = pair(scope, "r_w", [P, KT, ROUTED])
            r_bias = sb(scope, "r_bias", [P, ROUTED])

        with ExitStack() as scope:
            sb(scope, "pad4", [P, TT, D])
            eb_raw = sb(scope, "eb_raw", [ROUTED, D])
            eb_w = pair(scope, "eb_w", [ROUTED, D])
            r_log = sb(scope, "r_log", [P, TT, ROUTED])
            r_exp = sb(scope, "r_exp", [P, TT, ROUTED])
            r_sc = sb(scope, "r_sc", [P, TT, ROUTED])
            r_left = sb(scope, "r_left", [P, TT, ROUTED])
            r_dense = sb(scope, "r_dense", [P, TT, ROUTED])
            r_top = sb(scope, "r_top", [P, TT, 8])
            r_stat = sb(scope, "r_stat", [P, 5, TT])
            r_T = [pair(scope, f"r_T{i}", [ROUTED, P]) for i in range(2)]

        banks = ctx.enter_context(nc.psum_tensor("banks", [P, 8, 512], F32))
        flat = banks[:, :, :].rearrange("p b n -> p (b n)")
        S = [flat[:, 1024 * i:1024 * i + KV] for i in range(2)]
        Y = [banks[:, i, :] for i in range(4)]
        T = [banks[:, 4 + i, :] for i in range(2)]
        G = [banks[:, 6 + i, :] for i in range(2)]

        slots = {"gu0": (gu_raw[0], gu0[0], "w_ffn0", (0, 1024)), "gu1": (gu_raw[1], gu0[1], "w_ffn0", (0, 1024)),
                 "dn0": (dn_raw[0], dn0[0], "w_ffn0", (1024, 1536)), "dn1": (dn_raw[1], dn0[1], "w_ffn0", (1024, 1536)),
                 "kv": (raw_q, w_kv, None, (0, 1024)), "q": (raw_q, w_q, None, (0, 1024)),
                 "o": (raw_o, w_o, None, (0, 1024)),
                 "e0": (ex_raw[0], ex_w[0], "w_experts", (0, 2048)), "e1": (ex_raw[1], ex_w[1], "w_experts", (0, 2048))}

        def latents(h, kt, tt):
            return h[:, kt, tt // 2, SC + (tt % 2) * P:SC + (tt % 2) * P + P]

        def all_latents(h, kt):
            return h[:, kt, :, SC:KV]

        def keys(h, kt, n):
            return h[:, kt, n // 2, 384 * (n % 2):384 * (n % 2) + 384]

        def latents_all(h, tt):
            return h[:, :, tt // 2, SC + (tt % 2) * P:SC + (tt % 2) * P + P]

        def turned_weights(which, i, part, bank):
            if which < 2:
                dst = gu2[i % 2][part][:, :].rearrange("p (k n) -> p k n", k=KT)[:, :, which * P:which * P + P]
                return dst, bank.rearrange("p (k n) -> p k n", k=KT)
            return dn2[i % 2][part][:, :].rearrange("p (m r) -> p r m", r=4), bank.rearrange("p (r m) -> p r m", r=4)

        def crossed(step, part):
            if step[0] == "cq":
                return QC[part][:, step[1], :], bias_c[:, 0, step[1]:step[1] + 1]
            _, b, dt = step
            return KC[part][:, dt, b * SC:b * SC + SC], bias_c[:, 1, dt:dt + 1]

        def f32(ap):
            return ap.bitcast(F32)

        small_names = {n: i for i, n in enumerate(("s1", "z1", "s2", "z2", "gate", "up", "down"))}

        def sc(name):
            i = small_names[name]
            return small[:, i:i + 1]

        def slot_of(n, turn):
            return n // 2 if turn is None else n % 2

        def units_of(number):
            return 8 * LAYER[number // 2]["pairs"]

        def walk(c, eng, do):
            for number, block in enumerate(segments(blocks)):
                for turns, steps in block:
                    if turns == 1:
                        for s in steps:
                            do(s, number, None)
                            c.here.update(adds(s))
                    else:
                        with eng.Fori(0, turns) as turn:
                            c.enter(turn, steps)
                            for s in steps:
                                do(s, number, turn)
                                c.here.update(adds(s))
                        c.leave(turns)

        block = ctx.enter_context(nc.Block())

        @block.sync
        def _(sp):
            c = Counts()

            def row(i, per, turn):
                return i if turn is None else sp.snap(turn * per + i)

            def chunk(dram, at, lo, hi):
                return dram[bass.ds(at, 1), :, lo:hi].rearrange("a p n -> (a p) n")

            def do(step, number, turn):
                k = step[0]
                if k == "start":
                    sp.dma_start(small[:, :], ins["small"]).then_inc(sem("dma_small"), 16)
                    for b in range(B):
                        sp.dma_start(X[:, 2 * b:2 * b + 2, :], ins["x"][b].rearrange("(t p) d -> p t d", p=P))\
                            .then_inc(sem(f"dma_x{b}"), 16)
                    sp.dma_start(ctx_raw[:, :, :], ins["ctx"].rearrange("b (t p) d -> p (b t) d", p=P))\
                        .then_inc(sem("dma_ctx"), 16)
                elif k == "context":
                    sp.dma_start(ctxT_raw[:, :, :, :], ins["ctxT"]).then_inc(sem("dma_ctxT"), 16)
                    sp.dma_start(gate_raw[:, :, :], ins["gate_w"]).then_inc(sem("dma_gate"), 16)
                    sp.dma_start(qk_w[:, 0:2], ins["qk_norm"]).then_inc(sem("dma_qk"), 16)
                elif k == "w2load":
                    sp.dma_start(w2_raw[:, :, :], ins["w2"]).then_inc(sem("dma_w2"), 16)
                    sp.dma_start(w2_s[:, :, :], ins["s2"]).then_inc(sem("dma_w2"), 16)
                elif k == "x":
                    sp.wait_ge(sem("w2_ready"), 1)
                    sp.dma_start(x_raw[1][:, :], ins["w_cross"][1]).then_inc(sem("dma_xk"), 16)
                    sp.dma_start(bias_c[:, :, :], ins["b_cross"]).then_inc(sem("dma_bc"), 16)
                    sp.dma_start(x_raw[0][:, :], ins["w_cross"][0]).then_inc(sem("dma_xq"), 16)
                elif k == "c":
                    sp.wait_ge(sem("t_full"), c.at("t_full"))
                    sp.dma_start(c_raw[:, :, :], ins["ctx"].rearrange("b (t p) d -> p (b t) d", p=P))\
                        .then_inc(sem("dma_c"), 16)
                elif k == "begin" and number == 7:
                    sp.wait_ge(sem("xn"), c.at("xn"))
                    sp.dma_start(eb_raw[:, :], ins["expert_b"]).then_inc(sem("dma_eb"), 16)
                elif k == "router":
                    sp.wait_ge(sem("x_lo"), 2)
                    sp.dma_start(r_raw[:, :, :], ins["router_w"]).then_inc(sem("dma_r"), 16)
                    sp.dma_start(r_bias[:, :], ins["router_b"]).then_inc(sem("dma_rb"), 16)
                elif k in ("W", "H"):
                    _, slot, dma, i, per = step
                    raw, _, dram, (lo, hi) = slots[slot]
                    dram = ins[dram or ("w_attn1" if number <= 2 else "w_attn2")]
                    ring = RINGS[slot]
                    at = row(i, per, turn)
                    if number == 2 and ring == "e":
                        sp.wait_ge(sem("lo_rq"), c.at("lo_rq"))
                        sp.wait_ge(sem("lo_o"), c.at("lo_o"))
                    if number == 3 and slot == "e1" and i == 1 and turn is None:
                        sp.wait_ge(sem("xn"), c.at("xn"))
                    if number == 3 and ring != "e":
                        sp.wait_ge(sem("lo_e"), c.at("lo_e"))
                    if slot in ("kv", "q"):
                        if c.any("lo_rq"):
                            sp.wait_ge(sem("lo_rq"), c.at("lo_rq"))
                    else:
                        back = -1 if ring in ("gu", "dn", "e") else 0
                        if c.any("lo_" + ring, back):
                            sp.wait_ge(sem("lo_" + ring), c.at("lo_" + ring, back))
                    sp.dma_start(raw[:, :], chunk(dram, at, lo, hi)).then_inc(sem(dma), 16)
                elif k == "DQ":
                    _, i, per = step
                    at = row(i, per, turn)
                    if number == 4:
                        sp.wait_ge(sem("g_full"), c.at("g_full"))
                        sp.wait_ge(sem("lo_rq"), c.at("lo_rq"))
                        sp.wait_ge(sem("lo_o"), c.at("lo_o"))
                    if c.any("dq", -1):
                        sp.wait_ge(sem("dq"), c.at("dq", -1))
                    d = sem(f"dma_w13_{i % 2}")
                    sp.dma_start(w13_raw[i % 2][:, :, :].rearrange("p a g -> p (a g)"),
                                 ins["w13"][bass.ds(at, 1)].rearrange("a p n -> (a p) n")).then_inc(d, 16)
                    sp.dma_start(w13_s[i % 2][:, :, :].rearrange("p a g -> p (a g)"),
                                 ins["s13"][bass.ds(at, 1)].rearrange("a p n -> (a p) n")).then_inc(d, 16)

            walk(c, sp, do)
            for tt in range(TT):
                sp.wait_ge(sem("g_done"), c.at("g_done", tt + 1 - TT))
                sp.dma_start(out[tt // 2, (tt % 2) * P:(tt % 2) * P + P, :], X[:, tt, :]).then_inc(sem("dma_out"), 16)
            sp.wait_ge(sem("dma_out"), 16 * TT)

        @block.tensor
        def _(pe):
            c = Counts()

            def mm3(o, a, b, start, stop):
                nc.tensor.matmul(o, a[0], b[0], start=start, stop=False)
                nc.tensor.matmul(o, a[0], b[1], start=False, stop=False)
                return nc.tensor.matmul(o, a[1], b[0], start=False, stop=stop)

            k_sq_at = [None] * 4
            turned_at = [None]
            heads_out = [None]

            def over(pair_, f):
                return tuple(f(t) for t in pair_)

            def do(step, number, turn):
                k = step[0]
                if k in ("xnT", "xqT"):
                    tt = step[1]
                    if tt == 0:
                        pe.wait_ge(sem("const"), 1)
                    pe.wait_ge(sem("xn"), TT * number + tt + 1)
                    pe.wait_ge(sem("t_done"), c.at("t_done", -1))
                    t = T[c.even("t_full")]
                    for kt in range(KT):
                        m = nc.tensor.transpose(t[:, kt * P:kt * P + P], xn[:, tt, kt * P:kt * P + P], ident[:, :])
                    m.then_inc(sem("t_full"), 1)
                elif k == "sums":
                    b = step[1]
                    pe.wait_ge(sem("cq"), b + 1)
                    for kt in range(SC // P):
                        m = nc.tensor.matmul(Y[b], ones_bf[:, :], ctx_q[:, b * 4 + kt, :], start=kt == 0, stop=kt == 3)
                    m.then_inc(sem("csum"), 1)
                    if b == 0:
                        pe.wait_ge(sem("t_done"), c.at("t_done"))
                        for tt in range(TT):
                            for kt in range(KT):
                                m = nc.tensor.matmul(Y[2][:, 2 * tt:2 * tt + 2], xq_T[:, kt, tt * P:tt * P + P],
                                                     ones_bf[:, 0:2], start=kt == 0, stop=kt == KT - 1)
                        m.then_inc(sem("rowsum"), 1)
                elif k == "qmm":
                    tt = step[1]
                    pe.wait_ge(sem("g_done"), c.at("g_done", -1))
                    g = G[c.even("g_full")]
                    for kt in range(KT):
                        m = nc.tensor.matmul(g, xq_T[:, kt, tt * P:tt * P + P], ctx_q[:, (tt // 2) * 4 + kt, :],
                                             start=kt == 0, stop=kt == KT - 1)
                    m.then_inc(sem("g_full"), 1)
                elif k == "zeroY":
                    for tt in range(TT):
                        nc.tensor.matmul(Y[tt], zeros_bf[:, 0:P], zeros_bf[:, :], start=True, stop=False)
                elif k == "GU":
                    i = step[1]
                    w = gu0[i % 2] if number == 1 else gu2[i % 2]
                    if number == 1:
                        pe.wait_ge(sem("lo_gu"), c.at("lo_gu", i + 1 - min(i + 2, IT)))
                        if i == 0:
                            pe.wait_ge(sem("t_done"), c.at("t_done"))
                    else:
                        pe.wait_ge(sem("t_done"), c.at("t_done", (-2, 0)[i] if i <= 1 else -1))
                    for job, off in ((0, 0), (1, P)):
                        pe.wait_ge(sem("g_done"), c.at("g_done", job - 1))
                        g = G[c.even("g_full", job)]
                        for kt in range(KT):
                            a = over(w, lambda t: t[:, kt * 256 + off:kt * 256 + off + P])
                            m = mm3(g, a, over(H, lambda h: all_latents(h, kt)), kt == 0, kt == KT - 1)
                        m.then_inc(sem("g_full"), 1)
                elif k == "D":
                    i = step[1]
                    w = dn0[i % 2] if number == 1 else dn2[i % 2]
                    pe.wait_ge(sem("inner"), c.at("inner", 0 if i == IT - 1 else -1))
                    if number == 1:
                        pe.wait_ge(sem("lo_dn"), c.at("lo_dn", i + 1 - min(i + 2, IT)))
                    elif i in (0, IT - 1):
                        pe.wait_ge(sem("t_done"), c.at("t_done"))
                    for tt in range(TT):
                        m = mm3(Y[tt], over(inner0[i % 2] if number == 1 else inner2[i % 2], lambda t: t[:, tt * P:tt * P + P]),
                                over(w, lambda t: t[:, :]), False, i == IT - 1)
                        if i == IT - 1:
                            m.then_inc(sem("y_full"), 1)
                    if i < IT - 1:
                        m.then_inc(sem("d_full"), 1)
                elif k == "K":
                    n, rms = step[1:]
                    if n == 0:
                        pe.wait_ge(sem("lo_rq"), c.at("lo_rq"))
                        pe.wait_ge(sem("ctx_lo"), KT)
                    if n == 1 and turn is None:
                        pe.wait_ge(sem("t_done"), c.at("t_done", -1 if rms else 0))
                    pe.wait_ge(sem("g_done"), c.at("g_done", -1))
                    if rms:
                        k_sq_at[n] = c.at("k_sq", 1)
                    g = G[c.even("g_full")]
                    for kt in range(KT):
                        m = mm3(g[:, 0:384], over(w_kv, lambda t: t[:, kt * 256:kt * 256 + P]),
                                over(H, lambda h: keys(h, kt, n)), kt == 0, kt == KT - 1)
                    m.then_inc(sem("g_full"), 1)
                elif k == "KN":
                    n = step[1]
                    pe.wait_ge(sem("k_sq"), k_sq_at[n])
                    pe.wait_ge(sem("t_done"), c.at("t_done", -1))
                    t = T[c.even("t_full")]
                    nc.tensor.matmul(t[:, 0:384], ones[:, :], k_sq[slot_of(n, turn)], start=True, stop=True)\
                        .then_inc(sem("t_full"), 1)
                elif k == "q":
                    _, j, h, rms = step
                    if h == 0:
                        pe.wait_ge(sem("lo_rq"), c.at("lo_rq"))
                    pe.wait_ge(sem("g_done"), c.at("g_done", -1))
                    g = G[c.even("g_full")]
                    for kt in range(KT):
                        m = mm3(g, over(w_q, lambda t: t[:, kt * 256 + h * P:kt * 256 + h * P + P]),
                                over(H, lambda t: all_latents(t, kt)), kt == 0, kt == KT - 1)
                    m.then_inc(sem("g_full"), 1)
                elif k == "QN":
                    pe.wait_ge(sem("q_sq"), c.at("q_sq"))
                    pe.wait_ge(sem("g_done"), c.at("g_done", -1))
                    g = G[c.even("g_full")]
                    for i in range(8):
                        m = nc.tensor.matmul(g[:, i:i + 1], q_sq[i // 4][:, (i % 4) * P:(i % 4) * P + P], ones[:, 0:1],
                                             start=True, stop=True)
                    m.then_inc(sem("g_full"), 1)
                elif k == "V":
                    n = step[1]
                    pe.wait_ge(sem("g_done"), c.at("g_done", -1))
                    g = G[c.even("g_full")]
                    for kt in range(KT):
                        m = mm3(g[:, 0:384], over(w_kv, lambda t: t[:, kt * 256 + P:kt * 256 + 2 * P]),
                                over(H, lambda h: keys(h, kt, n)), kt == 0, kt == KT - 1)
                    m.then_inc(sem("g_full"), 1)
                elif k == "VT":
                    n = step[1]
                    pe.wait_ge(sem("g_done"), c.at("g_done", 0 if n == 2 else -1))
                    pe.wait_ge(sem("t_done"), c.at("t_done", -1))
                    t = T[c.even("t_full")]
                    for m_ in range(3):
                        m = nc.tensor.transpose(t[:, m_ * P:m_ * P + P], vT[n % 2][:, m_ * P:m_ * P + P], ident[:, :])
                    m.then_inc(sem("t_full"), 1)
                elif k == "S":
                    u = step[1]
                    j, r = divmod(u, 8)
                    b, h, qt = r // 4, (r // 2) % 2, r % 2
                    if u == 0:
                        pe.wait_ge(sem("g_done"), c.at("g_done", -2))
                        if number == 4:
                            pe.wait_ge(sem("k_lo"), c.at("k_lo"))
                    if r == 0 and u:
                        pe.wait_ge(sem("g_done"), c.at("g_done", -1))
                    if u >= 2:
                        pe.wait_ge(sem("exp"), c.at("exp", -1))
                    s = S[u % 2]
                    q0 = (b * 2 + qt) * P
                    a = over(QX[j % 2], lambda t: t[:, h, q0:q0 + P])
                    for lo, hi in ((0, 512), (512, KV)):
                        m = mm3(s[:, lo:hi], a, over(KX, lambda t: t[:, b * KV + lo:b * KV + hi]), True, True)
                    m.then_inc(sem("s_full"), 1)
                elif k == "T":
                    u = step[1]
                    ahead = min(1, units_of(number) - 1 - u)
                    pe.wait_ge(sem("p_ready"), c.at("p_ready", -ahead))
                    if u % 4 == 3:
                        turned_at[0] = c.at("t_done", 2)
                    for half in range(2):
                        pe.wait_ge(sem("t_done"), c.at("t_done", half - 1))
                        t = T[c.even("t_full", half)]
                        for m_ in range(3):
                            kk = (3 * half + m_) * P
                            m = nc.tensor.transpose(t[:, m_ * P:m_ * P + P], prob[u % 2][:, kk:kk + P], ident[:, :])
                        m.then_inc(sem("t_full"), 1)
                elif k == "PV":
                    n = step[1]
                    b = n % 2
                    pe.wait_ge(sem("t_done"), turned_at[0])
                    pe.wait_ge(sem("g_done"), c.at("g_done", -1))
                    heads_out[0] = c.at("g_done", 1)
                    g = G[c.even("g_full")]
                    for kt in range(KVT):
                        m = mm3(g, over(VX, lambda t: t[:, b * KVT + kt, :]), over(PT[n % 2], lambda t: t[:, kt, :]),
                                kt == 0, kt == KVT - 1)
                    m.then_inc(sem("g_full"), 1)
                elif k == "Wo":
                    tt = step[1]
                    if tt in (0, 2):
                        pe.wait_ge(sem("g_done"), heads_out[0])
                        pe.wait_ge(sem("lo_o"), c.at("lo_o"))
                    pe.wait_ge(sem("g_done"), c.at("g_done", -1))
                    g = G[c.even("g_full")]
                    for h in range(2):
                        m = mm3(g, over(OX, lambda t: t[:, h, tt * P:tt * P + P]),
                                over(w_o, lambda t: t[:, h * D:h * D + D]), h == 0, h == 1)
                    m.then_inc(sem("g_full"), 1)
                elif k == "gate":
                    tt = step[1]
                    if tt == 0:
                        pe.wait_ge(sem("gate_split"), 1)
                        pe.wait_ge(sem("t_done"), c.at("t_done"))
                    pe.wait_ge(sem("g_done"), c.at("g_done", -1))
                    g = G[c.even("g_full")]
                    for kt in range(KT):
                        m = mm3(g[:, 0:EXPERTS], over(H, lambda t: latents(t, kt, tt)), over(gate_w, lambda t: t[:, kt, :]),
                                kt == 0, kt == KT - 1)
                    m.then_inc(sem("g_full"), 1)
                elif k == "E":
                    _, e, tt, per = step
                    if tt == 0:
                        pe.wait_ge(sem("lo_e"), c.at("lo_e", e + 1 - min(e + 2, EXPERTS)))
                    pe.wait_ge(sem("g_done"), c.at("g_done", -1))
                    g = G[c.even("g_full")]
                    for kt in range(KT):
                        m = mm3(g, over(H, lambda t: latents(t, kt, tt)), over(ex_w[e % 2], lambda t: t[:, kt * D:kt * D + D]),
                                kt == 0, kt == KT - 1)
                    m.then_inc(sem("g_full"), 1)
                elif k == "TW":
                    which, i = step[1], step[2]
                    pe.wait_ge(sem("t_done"), c.at("t_done", -1))
                    t = T[c.even("t_full")]
                    if which == 0:
                        pe.wait_ge(sem("dq"), c.at("dq"))
                    if which == 2:
                        pe.wait_ge(sem("cut"), c.at("cut"))
                    for m_ in range(4):
                        src = w13_nat[:, 4 * which + m_, :, :].rearrange("p a g -> p (a g)") if which < 2 else w2_cut[:, m_, :]
                        m = nc.tensor.transpose(t[:, m_ * P:m_ * P + P], src, ident[:, :])
                    m.then_inc(sem("t_full"), 1)
                elif k in ("cq", "ck"):
                    b, dt = (0, step[1]) if k == "cq" else step[1:]
                    which = 0 if k == "cq" else 1
                    if k == "cq" and dt == 0:
                        pe.wait_ge(sem("t_done"), c.at("t_done"))
                    pe.wait_ge(sem("x_lo"), 1 if k == "ck" else 2)
                    pe.wait_ge(sem("g_done"), c.at("g_done", -1))
                    g = G[c.even("g_full")]
                    for kt in range(KT):
                        m = mm3(g, over(x_w[which], lambda t: t[:, kt * D + dt * P:kt * D + dt * P + P]),
                                over(H, lambda t: all_latents(t, kt) if k == "cq" else t[:, kt, b, 0:SC]),
                                kt == 0, kt == KT - 1)
                    m.then_inc(sem("g_full"), 1)
                elif k == "cs":
                    tt = step[1]
                    if tt == 0:
                        pe.wait_ge(sem("g_done"), c.at("g_done"))
                    if tt >= 2:
                        pe.wait_ge(sem("c_exp"), tt - 1)
                    for dt in range(KT):
                        m = mm3(Y[tt % 2], over(QC, lambda t: t[:, dt, tt * P:tt * P + P]),
                                over(KC, lambda t: t[:, dt, (tt // 2) * SC:(tt // 2) * SC + SC]), dt == 0, dt == KT - 1)
                    m.then_inc(sem("c_full"), 1)
                elif k == "ct":
                    tt = step[1]
                    pe.wait_ge(sem("c_exp"), tt + 1)
                    pe.wait_ge(sem("t_done"), c.at("t_done", -1))
                    t = T[c.even("t_full")]
                    for m_ in range(4):
                        m = nc.tensor.transpose(t[:, m_ * P:m_ * P + P], prob_c[tt % 2][:, m_ * P:m_ * P + P], ident[:, :])
                    m.then_inc(sem("t_full"), 1)
                elif k == "cpv":
                    tt = step[1]
                    pe.wait_ge(sem("t_done"), c.at("t_done", 0 if tt == TT - 1 else -1))
                    if tt == 0:
                        pe.wait_ge(sem("x_lo"), 3)
                    pe.wait_ge(sem("g_done"), c.at("g_done", -1))
                    g = G[c.even("g_full")]
                    for kt in range(4):
                        m = mm3(g, over(PC[tt % 2], lambda t: t[:, kt, :]),
                                over(c_w, lambda t: t[:, (tt // 2) * 4 + kt, :]), kt == 0, kt == 3)
                    m.then_inc(sem("g_full"), 1)
                elif k == "rl":
                    tt = step[1]
                    if tt == 0:
                        pe.wait_ge(sem("t_done"), c.at("t_done"))
                        pe.wait_ge(sem("r_lo"), 1)
                    pe.wait_ge(sem("g_done"), c.at("g_done", -1))
                    g = G[c.even("g_full")]
                    for kt in range(KT):
                        m = mm3(g[:, 0:ROUTED], over(H, lambda t: latents(t, kt, tt)), over(r_w, lambda t: t[:, kt, :]),
                                kt == 0, kt == KT - 1)
                    m.then_inc(sem("g_full"), 1)
                elif k == "rt":
                    tt = step[1]
                    pe.wait_ge(sem("r_dense"), tt // 2 + 1)
                    pe.wait_ge(sem("t_done"), c.at("t_done", -1))
                    t = T[c.even("t_full")]
                    nc.tensor.transpose(t[0:ROUTED, 0:P], r_dense[:, tt, :], ident[:, :]).then_inc(sem("t_full"), 1)
                elif k == "rm":
                    tt = step[1]
                    pe.wait_ge(sem("t_done"), c.at("t_done", tt % 2 - 1))
                    pe.wait_ge(sem("r_lo"), 2)
                    pe.wait_ge(sem("g_done"), c.at("g_done", -1))
                    g = G[c.even("g_full")]
                    mm3(g, over(r_T[tt % 2], lambda t: t[:, :]), over(eb_w, lambda t: t[:, :]), True, True)\
                        .then_inc(sem("g_full"), 1)

            walk(c, pe, do)

        @block.scalar
        def _(act):
            c = Counts()
            copy = nc.scalar.activation

            def do(step, number, turn):
                k = step[0]
                if k == "start":
                    nc.scalar.preload_act_table(ACT.Silu)
                elif k == "scale":
                    b = step[1]
                    if b == 0:
                        act.wait_ge(sem("derived"), 1)
                        act.wait_ge(sem("dma_ctx"), 16)
                    rows = slice(4 * b, 4 * b + 4)
                    copy(ctx_raw[:, rows, :], ctx_raw[:, rows, :], ACT.Identity, bias=sc("z2"), scale=derived[:, 1:2])\
                        .then_inc(sem("scaled"), 1)
                elif k == "xqT":
                    tt = step[1]
                    act.wait_ge(sem("t_full"), c.at("t_full", 1))
                    copy(xq_T[:, :, tt * P:tt * P + P], T[c.even("t_full")].rearrange("p (k n) -> p k n", k=KT), ACT.Copy)\
                        .then_inc(sem("t_done"), 1)
                elif k == "context":
                    act.wait_ge(sem("dma_ctxT"), 16)
                    for kt in range(KT):
                        copy(H[0][:, kt, :, 0:SC], ctxT_raw[:, kt, :, :], ACT.Copy).then_inc(sem("ctx_hi"), 1)
                elif k == "begin":
                    if number == 5:
                        nc.scalar.preload_act_table(ACT.Silu)
                    elif number in (2, 3, 6):
                        nc.scalar.preload_act_table(ACT.Exp)
                    elif number == 4:
                        nc.scalar.preload_act_table_set("natural_log_exp_and_others")
                elif k == "split":
                    _, name, which = step
                    act.wait_ge(sem("g_full"), c.at("g_full"))
                    if name == "xk":
                        act.wait_ge(sem("dq"), c.at("dq"))
                        act.wait_ge(sem("t_full"), c.at("t_full"))
                    act.wait_ge(sem("dma_" + name), 16)
                    if name == "c":
                        copy(c_w[0][:, :, :], c_raw[:, :, :], ACT.Copy).then_inc(sem("x_hi"), 1)
                    else:
                        copy(x_w[which][0][:, :], x_raw[which][:, :], ACT.Copy).then_inc(sem("x_hi"), 1)
                elif k in ("W", "H"):
                    slot, dma = step[1], step[2]
                    raw, w = slots[slot][:2]
                    ring = RINGS[slot]
                    users = "d_full" if ring == "dn" else "g_full"
                    if c.any(users):
                        act.wait_ge(sem(users), c.at(users))
                    act.wait_ge(sem(dma), c.at(dma, 16))
                    copy(w[0][:, :], raw[:, :], ACT.Copy).then_inc(sem("hi_" + ring), 1)
                elif k == "xnT":
                    tt = step[1]
                    act.wait_ge(sem("t_full"), c.at("t_full", 1))
                    src = T[c.even("t_full")].rearrange("p (k n) -> p k n", k=KT)
                    copy(latents_all(H[0], tt), src, ACT.Copy).then_inc(sem("hi"), 1)
                elif k == "GU":
                    i = step[1]
                    gated, silu, inner = (gated0, silu0, inner0) if number == 1 else (gated2, silu2, inner2)
                    act.wait_ge(sem("g_full"), c.at("g_full", 1))
                    copy(silu[:, :], G[0], ACT.Silu, scale=sc("gate") if number == 1 else 1.0).then_inc(sem("silu"), 1)
                    act.wait_ge(sem("g_done"), c.at("g_done", 2))
                    copy(inner[i % 2][0][:, :], gated[:, :], ACT.Copy).then_inc(sem("hi"), 1)
                elif k == "K":
                    n, rms = step[1:]
                    act.wait_ge(sem("g_full"), c.at("g_full", 1))
                    g = G[c.even("g_full")][:, 0:384]
                    if rms:
                        copy(k_sq[slot_of(n, turn)], g, ACT.Square).then_inc(sem("k_sq"), 1)
                    else:
                        copy(KX[0][:, 384 * n:384 * n + 384], g, ACT.Copy).then_inc(sem("hi"), 1)
                elif k == "KN":
                    n = step[1]
                    act.wait_ge(sem("t_done"), c.at("t_done", 1))
                    copy(k_r[slot_of(n, turn)][:, :], k_r[slot_of(n, turn)][:, :], ACT.Ln).then_inc(sem("k_ln"), 1)
                    act.wait_ge(sem("k_ln"), c.at("k_ln", 1))
                    copy(k_r[slot_of(n, turn)][:, :], k_r[slot_of(n, turn)][:, :], ACT.Exp, scale=-0.5).then_inc(sem("k_r"), 1)
                elif k == "KM":
                    n = step[1]
                    act.wait_ge(sem("k_raw"), c.at("k_raw", 1))
                    copy(KX[0][:, 384 * n:384 * n + 384], k_raw[n][:, :], ACT.Copy).then_inc(sem("hi"), 1)
                elif k == "q":
                    _, j, h, rms = step
                    act.wait_ge(sem("g_full"), c.at("g_full", 1))
                    g = G[c.even("g_full")]
                    if rms:
                        copy(q_sq[h][:, :], g, ACT.Square).then_inc(sem("q_sq"), 1)
                    copy(QX[j % 2][0][:, h, :], g, ACT.Copy, scale=HD ** -0.5).then_inc(sem("hi"), 1)
                elif k == "VT":
                    n = step[1]
                    act.wait_ge(sem("t_full"), c.at("t_full", 1))
                    copy(VX[0][:, 3 * n:3 * n + 3, :].rearrange("p k n -> p (k n)"), T[c.even("t_full")][:, 0:384],
                         ACT.Copy).then_inc(sem("hi"), 1)
                elif k == "X":
                    u = step[1]
                    j, r = divmod(u, 8)
                    act.wait_ge(sem("bias"), c.at("bias"))
                    col = (r // 2 % 2) * 4 + (r // 4) * 2 + r % 2
                    scale = rq[j % 2][:, col:col + 1] if number == 4 else 1.0
                    copy(prob[u % 2][:, :], S[u % 2], ACT.Exp, bias=nbias[:, u % 4:u % 4 + 1], scale=scale,
                         accum_out=rsum[:, u % 4:u % 4 + 1]).then_inc(sem("exp"), 1)
                elif k == "T":
                    u = step[1]
                    for half in range(2):
                        act.wait_ge(sem("t_full"), c.at("t_full", half + 1))
                        src = T[c.even("t_full", half)][:, 0:384].rearrange("p (k n) -> p k n", k=3)
                        copy(PT[u // 4 % 2][0][:, 3 * half:3 * half + 3, (u % 4) * P:(u % 4) * P + P], src,
                             ACT.Copy).then_inc(sem("hi"), 1)
                elif k == "PV":
                    b = step[1] % 2
                    act.wait_ge(sem("g_full"), c.at("g_full", 1))
                    copy(OX[0][:, :, b * SQ:b * SQ + SQ], G[c.even("g_full")].rearrange("p (h n) -> p h n", h=2),
                         ACT.Copy).then_inc(sem("hi"), 1)
                elif k == "TW":
                    which, i = step[1], step[2]
                    act.wait_ge(sem("t_full"), c.at("t_full", 1))
                    dst, src = turned_weights(which, i, 0, T[c.even("t_full")])
                    copy(dst, src, ACT.Copy).then_inc(sem("hi"), 1)
                elif k == "gate" and step[1] == TT - 1:
                    act.wait_ge(sem("e_bias"), 1)
                    for tt in range(TT):
                        copy(e_exp[:, tt, :], padded[:, tt, 6:WIDE], ACT.Exp, bias=ntop[:, tt:tt + 1])\
                            .then_inc(sem("e_exp"), 1)
                elif k in ("cq", "ck"):
                    if step == ("ck", 0, 0):
                        act.wait_ge(sem("dma_bc"), 16)
                    act.wait_ge(sem("g_full"), c.at("g_full", 1))
                    dst, bias = crossed(step, 0)
                    copy(dst, G[c.even("g_full")], ACT.Identity, bias=bias).then_inc(sem("hi"), 1)
                elif k == "cs":
                    tt = step[1]
                    act.wait_ge(sem("c_bias"), tt + 1)
                    copy(prob_c[tt % 2][:, :], Y[tt % 2], ACT.Exp, bias=stat_c[:, 1, tt:tt + 1], scale=D ** -0.5,
                         accum_out=stat_c[:, 2, tt:tt + 1]).then_inc(sem("c_exp"), 1)
                elif k == "ct":
                    act.wait_ge(sem("t_full"), c.at("t_full", 1))
                    copy(PC[step[1] % 2][0][:, :, :].rearrange("p k n -> p (k n)"), T[c.even("t_full")], ACT.Copy)\
                        .then_inc(sem("hi"), 1)
                elif k == "top":
                    act.wait_ge(sem("r_bias"), step[1] + 1)
                    for tt in (2 * step[1], 2 * step[1] + 1):
                        copy(r_exp[:, tt, :], r_log[:, tt, :], ACT.Exp, bias=r_stat[:, 1, tt:tt + 1],
                             accum_out=r_stat[:, 2, tt:tt + 1]).then_inc(sem("r_exp"), 1)
                elif k == "rt":
                    act.wait_ge(sem("t_full"), c.at("t_full", 1))
                    copy(r_T[step[1] % 2][0][:, :], T[c.even("t_full")][0:ROUTED, 0:P], ACT.Copy).then_inc(sem("hi"), 1)

            walk(c, act, do)

        @block.vector
        def _(dve):
            c = Counts()
            chained = [0]

            def chain(ins):
                chained[0] += 1
                ins.then_inc(sem("dve"), 1)
                dve.wait_ge(sem("dve"), chained[0])

            ts, tt_, stt = nc.vector.tensor_scalar, nc.vector.tensor_tensor, nc.vector.scalar_tensor_tensor

            def split_lo(dst, src, hi_, done, name="hi", more=1):
                dve.wait_ge(sem(name), c.at(name, more))
                tt_(dst, src, f32(hi_), ALU.subtract).then_inc(sem(done), 1)

            def rounded(dst, src, last):
                chain(ts(src, src, 0.0, 255.0, ALU.max, ALU.min))
                last(ts(dst, src, ROUND, ROUND + MID, ALU.add, ALU.subtract))

            def do(step, number, turn):
                k = step[0]
                if k == "start":
                    dve.sem_inc(sem("g_done"), 2)
                    dve.sem_inc(sem("t_done"), 2)
                    dve.wait_ge(sem("dma_small"), 16)
                    d = derived
                    nc.vector.reciprocal(d[:, 0:1], sc("s1"))
                    nc.vector.reciprocal(d[:, 1:2], sc("s2"))
                    ts(d[:, 2:3], sc("z1"), -1.0, MID, ALU.mult, ALU.add)
                    ts(d[:, 3:4], sc("z2"), -1.0, MID, ALU.mult, ALU.add)
                    chain(tt_(d[:, 4:5], sc("s1"), sc("s2"), ALU.mult))
                    stt(d[:, 5:6], d[:, 2:3], float(SC), d[:, 3:4], ALU.mult, ALU.mult).then_inc(sem("derived"), 1)
                    dve.wait_ge(sem("derived"), 1)
                elif k == "bn":
                    _, n, tt = step
                    if n == 0:
                        dve.wait_ge(sem(f"dma_x{tt // 2}"), 16)
                    else:
                        dve.wait_ge(sem("g_done"), c.at("g_done"))
                    chain(nc.vector.bn_stats(moments[:, tt, :], X[:, tt, :]))
                    chain(nc.vector.bn_aggr(mean_var[:, tt, :], moments[:, tt, :]))
                    ts(var[:, tt:tt + 1], mean_var[:, tt, 1:2], 1e-5, None, ALU.add).then_inc(sem("var"), 1)
                elif k == "xn":
                    _, n, tt = step
                    dve.wait_ge(sem("rstd"), TT * n + tt + 1)
                    i_ = ts(xn[:, tt, :], X[:, tt, :], mean_var[:, tt, 0:1], rstd[:, tt:tt + 1], ALU.subtract, ALU.mult)
                    if n:
                        i_.then_inc(sem("xn"), 1)
                    else:
                        chain(i_)
                        chain(ts(xn[:, tt, :], xn[:, tt, :], derived[:, 0:1], sc("z1"), ALU.mult, ALU.add))
                        rounded(xn[:, tt, :], xn[:, tt, :], lambda i_: i_.then_inc(sem("xn"), 1))
                elif k == "quantise":
                    b = step[1]
                    rows = slice(4 * b, 4 * b + 4)
                    dve.wait_ge(sem("scaled"), b + 1)
                    rounded(ctx_q[:, rows, :], ctx_raw[:, rows, :], lambda i_: i_.then_inc(sem("cq"), 1))
                elif k == "begin":
                    if number == 2:
                        dve.wait_ge(sem("dma_qk"), 16)
                        chain(tt_(qk_w[:, 2:3], qk_w[:, 0:1], qk_w[:, 1:2], ALU.mult))
                    if number == 3:
                        chain(nc.vector.memset(padded[:, :, 0:6], BIG))
                    if number == 5:
                        nc.vector.memset(w2_nat[:, 4 * INTER:], 0)
                        chain(nc.vector.memset(w2_half[:, 4 * INTER // HALF:], 0.0))
                elif k == "xnT":
                    tt = step[1]
                    split_lo(latents_all(H[1], tt), T[c.even("t_full")].rearrange("p (k n) -> p k n", k=KT),
                             latents_all(H[0], tt), "t_done")
                elif k == "sums":
                    b = step[1]
                    dve.wait_ge(sem("csum"), b + 1)
                    chain(ts(cz[:, b, :], Y[b], derived[:, 2:3], None, ALU.mult))
                    if b == 0:
                        dve.wait_ge(sem("rowsum"), 1)
                        chain(ts(row_bias[:, :], Y[2][:, 0:2 * TT:2], derived[:, 3:4], derived[:, 5:6], ALU.mult, ALU.add))
                elif k == "qmm":
                    tt = step[1]
                    dve.wait_ge(sem("g_full"), c.at("g_full", 1))
                    stt(q_tmp[:, :], G[c.even("g_full")], row_bias[:, tt:tt + 1], cz[:, tt // 2, :], ALU.add, ALU.add)\
                        .then_inc(sem("g_done"), 1)
                    dve.wait_ge(sem("g_done"), c.at("g_done", 1))
                    chain(stt(X[:, tt, :], q_tmp[:, :], derived[:, 4:5], X[:, tt, :], ALU.mult, ALU.add))
                elif k == "GU":
                    gated, silu = (gated0, silu0) if number == 1 else (gated2, silu2)
                    if c.any("inner"):
                        dve.wait_ge(sem("inner"), c.at("inner"))
                    dve.wait_ge(sem("silu"), c.at("silu", 1))
                    dve.wait_ge(sem("g_full"), c.at("g_full", 2))
                    stt(gated[:, :], G[1], sc("up") if number == 1 else 1.0, silu[:, :], ALU.mult, ALU.mult)\
                        .then_inc(sem("g_done"), 2)
                elif k == "Yadd":
                    tt = step[1]
                    dve.wait_ge(sem("y_full"), c.at("y_full", tt + 1 - TT))
                    chain(stt(X[:, tt, :], Y[tt], sc("down") if number == 1 else 1.0, X[:, tt, :], ALU.mult, ALU.add))
                elif k == "K":
                    n, rms = step[1:]
                    g = G[c.even("g_full")][:, 0:384]
                    cols = slice(384 * n, 384 * n + 384)
                    if rms:
                        dve.wait_ge(sem("k_sq"), c.at("k_sq", 1))
                        ts(k_raw[n][:, :], g, qk_w[:, 2:3], None, ALU.mult).then_inc(sem("g_done"), 1)
                    else:
                        split_lo(KX[1][:, cols], g, KX[0][:, cols], "g_done")
                elif k == "KN":
                    n = step[1]
                    dve.wait_ge(sem("t_full"), c.at("t_full", 1))
                    ts(k_r[slot_of(n, turn)][:, :], T[c.even("t_full")][:, 0:384], 1.0 / HD, 1e-6, ALU.mult, ALU.add)\
                        .then_inc(sem("t_done"), 1)
                elif k == "KM":
                    n = step[1]
                    dve.wait_ge(sem("k_r"), c.at("k_r"))
                    tt_(k_raw[n][:, :], k_raw[n][:, :], k_r[slot_of(n, turn)][:, :], ALU.mult).then_inc(sem("k_raw"), 1)
                elif k == "q":
                    _, j, h, rms = step
                    dve.wait_ge(sem("hi"), c.at("hi", 1))
                    stt(QX[j % 2][1][:, h, :], G[c.even("g_full")], HD ** -0.5, f32(QX[j % 2][0][:, h, :]), ALU.mult,
                        ALU.subtract).then_inc(sem("g_done"), 1)
                elif k == "QN":
                    dve.wait_ge(sem("g_full"), c.at("g_full", 1))
                    ts(qvar[:, :], G[c.even("g_full")][:, 0:8], 1.0 / HD, 1e-6, ALU.mult, ALU.add).then_inc(sem("g_done"), 1)
                elif k == "V":
                    n = step[1]
                    if number == 4 and n < 2:
                        dve.wait_ge(sem("k_lo"), c.at("k_lo", (-3, -1)[n]))
                    dve.wait_ge(sem("g_full"), c.at("g_full", 1))
                    nc.vector.tensor_copy(vT[n % 2][:, :], G[c.even("g_full")][:, 0:384]).then_inc(sem("g_done"), 1)
                elif k == "VT":
                    n = step[1]
                    flat_v = [v[:, 3 * n:3 * n + 3, :].rearrange("p k n -> p (k n)") for v in VX]
                    split_lo(flat_v[1], T[c.even("t_full")][:, 0:384], flat_v[0], "t_done")
                elif k == "S":
                    u = step[1]
                    j, r = divmod(u, 8)
                    col = (r // 2 % 2) * 4 + (r // 4) * 2 + r % 2
                    dve.wait_ge(sem("s_full"), c.at("s_full", 1))
                    nc.vector.reduce_max(top[:, u % 4:u % 4 + 1], S[u % 2], AX.X).then_inc(sem("s_max"), 1)
                    dve.wait_ge(sem("s_max"), c.at("s_max", 1))
                    if number == 4 and r == 0:
                        dve.wait_ge(sem("rq"), c.at("rq"))
                    scale = rq[j % 2][:, col:col + 1] if number == 4 else 1.0
                    ts(nbias[:, u % 4:u % 4 + 1], top[:, u % 4:u % 4 + 1], scale, -1.0, ALU.mult, ALU.mult)\
                        .then_inc(sem("bias"), 1)
                elif k == "R":
                    u = step[1]
                    dve.wait_ge(sem("exp"), c.at("exp"))
                    nc.vector.reciprocal(rinv[:, u % 4:u % 4 + 1], rsum[:, u % 4:u % 4 + 1]).then_inc(sem("rinv"), 1)
                elif k == "T":
                    u = step[1]
                    for half in range(2):
                        src = T[c.even("t_full", half)][:, 0:384].rearrange("p (k n) -> p k n", k=3)
                        hi_, lo_ = (t[:, 3 * half:3 * half + 3, (u % 4) * P:(u % 4) * P + P] for t in PT[u // 4 % 2])
                        split_lo(lo_, src, hi_, "t_done", more=half + 1)
                elif k == "PV":
                    b = step[1] % 2
                    hi_, lo_ = (t[:, :, b * SQ:b * SQ + SQ] for t in OX)
                    split_lo(lo_, G[c.even("g_full")].rearrange("p (h n) -> p h n", h=2), hi_, "g_done")
                elif k == "Wo":
                    tt = step[1]
                    dve.wait_ge(sem("g_full"), c.at("g_full", 1))
                    dve.wait_ge(sem("g_done"), c.at("g_done"))
                    tt_(X[:, tt, :], G[c.even("g_full")], X[:, tt, :], ALU.add).then_inc(sem("g_done"), 1)
                elif k == "gate":
                    tt = step[1]
                    dve.wait_ge(sem("g_full"), c.at("g_full", 1))
                    nc.vector.tensor_copy(padded[:, tt, 6:WIDE], G[c.even("g_full")][:, 0:EXPERTS]).then_inc(sem("g_done"), 1)
                    if tt == TT - 1:
                        dve.wait_ge(sem("g_done"), c.at("g_done", 1))
                        for t in range(TT):
                            i_ = nc.vector.max(top8[:, t, :], padded[:, t, :])
                        chain(i_)
                        ts(ntop[:, :], top8[:, :, 6], -1.0, None, ALU.mult).then_inc(sem("e_bias"), 1)
                        for t in range(TT):
                            i_ = nc.vector.match_replace(left[:, t, :], top8[:, t, :], padded[:, t, :], -BIG)
                        chain(i_)
                        dve.wait_ge(sem("e_exp"), TT)
                        ts(chosen[:, :, :], left[:, :, 6:WIDE], -BIG, None, ALU.is_le).then_inc(sem("dve"), 1)
                        chained[0] += 1
                        dve.wait_ge(sem("dve"), chained[0])
                        chain(tt_(e_exp[:, :, :], e_exp[:, :, :], chosen[:, :, :], ALU.mult))
                        chain(nc.vector.reduce_sum(e_sum[:, :], e_exp[:, :, :], AX.X))
                        chain(nc.vector.reciprocal(e_inv[:, :], e_sum[:, :]))
                        for t in range(TT):
                            i_ = ts(e_w[:, t, :], e_exp[:, t, :], e_inv[:, t:t + 1], None, ALU.mult)
                        chain(i_)
                elif k == "E":
                    _, e, tt, per = step
                    dve.wait_ge(sem("g_full"), c.at("g_full", 1))
                    dve.wait_ge(sem("g_done"), c.at("g_done"))
                    at = e if turn is None else turn * per + e
                    stt(X[:, tt, :], G[c.even("g_full")], e_w[:, tt, bass.ds(at, 1)], X[:, tt, :], ALU.mult, ALU.add)\
                        .then_inc(sem("g_done"), 1)
                elif k == "split" and step[1] == "xk":
                    split_lo(x_w[1][1][:, :], x_raw[1][:, :], x_w[1][0][:, :], "x_lo", "x_hi")
                elif k == "DQ2":
                    nibble = step[1]
                    if nibble == 0:
                        dve.wait_ge(sem("dma_w2"), 32)
                        chain(nc.vector.tensor_copy(
                            w2_half[:, 0:4 * INTER // HALF].rearrange("p (n h) -> p n h", h=2),
                            w2_s[:, :, :].rearrange("p r a -> p (r a)").unsqueeze(2).to_broadcast([P, 86, 2])))
                    nat = w2_nat[:, 0:4 * INTER].rearrange("p (r a g) -> p r a g", a=2, g=GROUP)[:, :, nibble, :]
                    chain(ts(nat, w2_raw[:, :, :], *NIBBLES[nibble]))
                    if nibble == 1:
                        dve.sem_inc(sem("w2_ready"), 1)
                elif k == "DQ":
                    i = step[1]
                    dve.wait_ge(sem("t_full"), c.at("t_full"))
                    dma = f"dma_w13_{i % 2}"
                    dve.wait_ge(sem(dma), c.at(dma, 32))
                    raw = w13_raw[i % 2][:, :, :]
                    ts(w13_nib[0][:, :, :], raw, 4, None, ALU.arith_shift_right)
                    ts(w13_nib[1][:, :, :], raw, 28, 28, ALU.logical_shift_left, ALU.arith_shift_right).then_inc(sem("nib"), 1)
                    dve.wait_ge(sem("nib"), c.at("nib", 1))
                    for nibble in range(2):
                        i_ = tt_(w13_nat[:, :, nibble, :], w13_nib[nibble][:, :, :],
                                 w13_s[i % 2][:, :, nibble:nibble + 1].to_broadcast([P, 2 * KT, GROUP]), ALU.mult)
                    i_.then_inc(sem("dq"), 1)
                elif k == "cut":
                    _, i, per = step
                    dve.wait_ge(sem("t_full"), c.at("t_full"))
                    at = i if turn is None else turn * per + i
                    for r in range(4):
                        halves = P // HALF
                        i_ = tt_(w2_cut[:, r, :].rearrange("p (n g) -> p n g", g=HALF),
                                 w2_nat[:, bass.ds(at * P + r * INTER, P)].rearrange("p (n g) -> p n g", g=HALF),
                                 w2_half[:, bass.ds(at * halves + r * INTER // HALF, halves)].unsqueeze(2)
                                 .to_broadcast([P, halves, HALF]), ALU.mult)
                    i_.then_inc(sem("cut"), 1)
                elif k == "TW":
                    _, which, i, per = step
                    hi_, src = turned_weights(which, i, 0, T[c.even("t_full")])
                    lo_, _ = turned_weights(which, i, 1, T[c.even("t_full")])
                    split_lo(lo_, src, hi_, "t_done")
                elif k in ("cq", "ck"):
                    dve.wait_ge(sem("hi"), c.at("hi", 1))
                    hi_, bias = crossed(step, 0)
                    lo_, _ = crossed(step, 1)
                    stt(lo_, G[c.even("g_full")], bias, f32(hi_), ALU.add, ALU.subtract).then_inc(sem("g_done"), 1)
                elif k == "cs":
                    tt = step[1]
                    dve.wait_ge(sem("c_full"), tt + 1)
                    chain(nc.vector.reduce_max(stat_c[:, 0, tt:tt + 1], Y[tt % 2], AX.X))
                    ts(stat_c[:, 1, tt:tt + 1], stat_c[:, 0, tt:tt + 1], -D ** -0.5, None, ALU.mult).then_inc(sem("c_bias"), 1)
                elif k == "ct":
                    hi_, lo_ = (t[:, :, :].rearrange("p k n -> p (k n)") for t in PC[step[1] % 2])
                    split_lo(lo_, T[c.even("t_full")], hi_, "t_done")
                elif k == "cpv":
                    tt = step[1]
                    dve.wait_ge(sem("c_exp"), tt + 1)
                    chain(nc.vector.reciprocal(stat_c[:, 3, tt:tt + 1], stat_c[:, 2, tt:tt + 1]))
                    dve.wait_ge(sem("g_full"), c.at("g_full", 1))
                    stt(X[:, tt, :], G[c.even("g_full")], stat_c[:, 3, tt:tt + 1], X[:, tt, :], ALU.mult, ALU.add)\
                        .then_inc(sem("g_done"), 1)
                elif k == "rl":
                    tt = step[1]
                    if tt == 0:
                        dve.wait_ge(sem("dma_rb"), 16)
                    dve.wait_ge(sem("g_full"), c.at("g_full", 1))
                    tt_(r_log[:, tt, :], G[c.even("g_full")][:, 0:ROUTED], r_bias[:, :], ALU.add).then_inc(sem("g_done"), 1)
                elif k == "top":
                    rows = slice(2 * step[1], 2 * step[1] + 2)
                    dve.wait_ge(sem("g_done"), c.at("g_done"))
                    chain(nc.vector.reduce_max(r_stat[:, 0, rows], r_log[:, rows, :], AX.X))
                    ts(r_stat[:, 1, rows], r_stat[:, 0, rows], -1.0, None, ALU.mult).then_inc(sem("r_bias"), 1)
                elif k == "choose":
                    pair = (2 * step[1], 2 * step[1] + 1)
                    rows = slice(2 * step[1], 2 * step[1] + 2)
                    dve.wait_ge(sem("r_exp"), 2 * step[1] + 2)
                    chain(nc.vector.reciprocal(r_stat[:, 3, rows], r_stat[:, 2, rows]))
                    for tt in pair:
                        i_ = ts(r_sc[:, tt, :], r_exp[:, tt, :], r_stat[:, 3, tt:tt + 1], None, ALU.mult)
                    chain(i_)
                    for tt in pair:
                        i_ = nc.vector.max(r_top[:, tt, :], r_sc[:, tt, :])
                    chain(i_)
                    for tt in pair:
                        i_ = nc.vector.match_replace(r_left[:, tt, :], r_top[:, tt, :], r_sc[:, tt, :], -1.0)
                    chain(i_)
                    stt(r_dense[:, rows, :], r_left[:, rows, :], 0.0, r_sc[:, rows, :], ALU.is_lt, ALU.mult)\
                        .then_inc(sem("r_dense"), 1)
                    chain(nc.vector.reduce_sum(r_stat[:, 4, rows], r_top[:, rows, :], AX.X))
                elif k == "rx":
                    tt = step[1]
                    chain(stt(X[:, tt, :], xn[:, tt, :], r_stat[:, 4, tt:tt + 1], X[:, tt, :], ALU.mult, ALU.add))
                elif k == "rt":
                    hi_, lo_ = (t[:, :] for t in r_T[step[1] % 2])
                    split_lo(lo_, T[c.even("t_full")][0:ROUTED, 0:P], hi_, "t_done")
                elif k == "rm":
                    tt = step[1]
                    dve.wait_ge(sem("g_full"), c.at("g_full", 1))
                    tt_(X[:, tt, :], G[c.even("g_full")], X[:, tt, :], ALU.add).then_inc(sem("g_done"), 1)

            walk(c, dve, do)
            dve.wait_ge(sem("g_done"), c.at("g_done"))

        @block.gpsimd
        def _(pool):
            c = Counts()

            def hi_part(dst, src):
                return nc.gpsimd.tensor_scalar(dst, src, 1.0, 1.0, ALU.mult, ALU.mult)

            def lo_part(dst, src, hi_):
                return nc.gpsimd.tensor_tensor(dst, src, f32(hi_), ALU.subtract)

            def split(w, raw, own, done):
                hi_part(w[0], raw).then_inc(sem(own), 1)
                split_count[0] += 1
                pool.wait_ge(sem(own), split_count[0])
                lo_part(w[1], raw, w[0]).then_inc(sem(done), 1)

            split_count = [0]

            def do(step, number, turn):
                k = step[0]
                if k == "start":
                    nc.gpsimd.memset(neg_half[:, :], -0.5)
                    nc.gpsimd.memset(zeros_bf[:, :], 0.0)
                    nc.gpsimd.memset(ones_bf[:, :], 1.0)
                    nc.gpsimd.memset(ones[:, :], 1.0)
                    nc.gpsimd.memset(ident[:, :], 0.0).then_inc(sem("blank"), 1)
                    pool.wait_ge(sem("blank"), 1)
                    nc.gpsimd.affine_select(out=ident[:, :], in_=ident[:, :], compare_op=ALU.not_equal, fill=1.0, base=0,
                                            pattern=[[-1, P]], channel_multiplier=1).then_inc(sem("const"), 1)
                elif k == "bn":
                    _, n, tt = step
                    pool.wait_ge(sem("var"), TT * n + tt + 1)
                    nc.gpsimd.tensor_tensor(rstd[:, tt:tt + 1], var[:, tt:tt + 1], neg_half[:, 0:1], ALU.pow)\
                        .then_inc(sem("rstd"), 1)
                elif k == "lows":
                    for kt in range(KT):
                        pool.wait_ge(sem("ctx_hi"), kt + 1)
                        lo_part(H[1][:, kt, :, 0:SC], ctxT_raw[:, kt, :, :], H[0][:, kt, :, 0:SC]).then_inc(sem("ctx_lo"), 1)
                    pool.wait_ge(sem("dma_gate"), 16)
                    split((gate_w[0][:, :, :], gate_w[1][:, :, :]), gate_raw[:, :, :], "pool", "gate_split")
                elif k == "router":
                    pool.wait_ge(sem("dma_r"), 16)
                    split((r_w[0][:, :, :], r_w[1][:, :, :]), r_raw[:, :, :], "pool", "r_lo")
                elif k == "begin" and number == 7:
                    pool.wait_ge(sem("dma_eb"), 16)
                    split((eb_w[0][:, :], eb_w[1][:, :]), eb_raw[:, :], "pool", "r_lo")
                elif k in ("W", "L"):
                    raw, w = slots[step[1]][:2]
                    ring = RINGS[step[1]]
                    pool.wait_ge(sem("hi_" + ring), c.at("hi_" + ring, 0 if k == "L" else 1))
                    lo_part(w[1][:, :], raw[:, :], w[0][:, :]).then_inc(sem("lo_" + ring), 1)
                elif k == "GU":
                    i = step[1]
                    gated, inner = (gated0, inner0) if number == 1 else (gated2, inner2)
                    pool.wait_ge(sem("hi"), c.at("hi", 1))
                    lo_part(inner[i % 2][1][:, :], gated[:, :], inner[i % 2][0][:, :]).then_inc(sem("inner"), 1)
                elif k == "R":
                    u = step[1]
                    pool.wait_ge(sem("rinv"), c.at("rinv", 1))
                    pool.sem_inc(sem("p_begun"), 1)
                    nc.gpsimd.tensor_scalar(prob[u % 2][:, :], prob[u % 2][:, :], rinv[:, u % 4:u % 4 + 1], 1.0,
                                            ALU.mult, ALU.mult).then_inc(sem("p_ready"), 1)
                elif k == "KM":
                    n = step[1]
                    cols = slice(384 * n, 384 * n + 384)
                    pool.wait_ge(sem("hi"), c.at("hi", 1))
                    lo_part(KX[1][:, cols], k_raw[n][:, :], KX[0][:, cols]).then_inc(sem("k_lo"), 1)
                elif k == "QN":
                    j = step[1]
                    pool.wait_ge(sem("g_done"), c.at("g_done", 1))
                    nc.gpsimd.tensor_tensor(rq[j % 2][:, :], qvar[:, :], neg_half[:, :], ALU.pow).then_inc(sem("rq"), 1)
                elif k == "split" and step[1] != "xk":
                    w, raw = (c_w, c_raw[:, :, :]) if step[1] == "c" else (x_w[step[2]], x_raw[step[2]][:, :])
                    pool.wait_ge(sem("x_hi"), c.at("x_hi", 1))
                    whole = (slice(None),) * len(raw.shape)
                    lo_part(w[1][whole], raw, w[0][whole]).then_inc(sem("x_lo"), 1)

            walk(c, pool, do)


def kernel(**inputs):
    import numpy as np
    import concourse.bacc as _bacc
    from concourse import mybir as _mybir
    from concourse.bass_utils import run_bass_kernel_spmd as _run

    v = {k: np.asarray(a) for k, a in inputs.items()}

    def tiled(w):
        return w.reshape(-1, P, w.shape[-1]).transpose(1, 0, 2)

    def attention_chunks(n, heads_kv):
        wq, wk, wv, wo = (v[f"L{n}_xattn_W{x}"] for x in "qkvo")
        pairs = HEADS // heads_kv // 2
        out = []
        for g in range(heads_kv):
            kv_cols = slice(g * HD, g * HD + HD)
            out.append(np.concatenate([tiled(wk[:, kv_cols]), tiled(wv[:, kv_cols])], axis=2).reshape(P, -1))
            for j in range(pairs):
                q_cols = slice((g * pairs + j) * 2 * HD, (g * pairs + j + 1) * 2 * HD)
                out.append(tiled(wq[:, q_cols]).reshape(P, -1))
                out.append(tiled(wo[q_cols, :]).reshape(P, -1))
        return np.stack(out)

    def padded_rows(w, n):
        return np.concatenate([w, np.zeros((n - w.shape[0], *w.shape[1:]), w.dtype)])

    gate_t, up_t = (tiled(padded_rows(v[f"L0_ffn_{x}_w"], IT * P).T) for x in ("gate", "up"))
    down_t = padded_rows(v["L0_ffn_down_w"].T, IT * P)
    ffn0 = [np.concatenate([np.concatenate([g[:, :, i * P:i * P + P] for g in (gate_t, up_t)], axis=2).reshape(P, -1),
                            down_t[i * P:i * P + P]], axis=1) for i in range(IT)]
    packed = [padded_rows(v[f"L2_ffn_w{i}"].reshape(INTER, KT * GROUP), IT * P).reshape(IT, P, KT * GROUP) for i in (1, 3)]
    scales = [padded_rows(v[f"L2_ffn_s{i}"].reshape(INTER, 2 * KT), IT * P).reshape(IT, P, 2 * KT) for i in (1, 3)]
    experts = v["L1_ffn_expert_w"].reshape(EXPERTS, KT, P, D).transpose(0, 2, 1, 3).reshape(EXPERTS, P, KT * D)
    small = [v[f"L0_xattn_{x}"] for x in ("x1_scale", "x1_zp", "x2_scale", "x2_zp")]
    small += [v[f"L0_ffn_{x}_scale"] for x in ("gate", "up", "down")]
    c4 = v["ctx_4096"]
    arrays = {
        "x": v["x"],
        "ctx": c4,
        "ctxT": c4.transpose(2, 0, 1).reshape(KT, P, B, SC).transpose(1, 0, 2, 3),
        "small": np.broadcast_to(np.stack([a.reshape(()) for a in small]), (P, 7)),
        "w_ffn0": np.stack(ffn0),
        "w_attn1": attention_chunks(1, LAYER[1]["kv"]),
        "w_attn2": attention_chunks(2, LAYER[2]["kv"]),
        "qk_norm": np.stack([v["L2_xattn_q_norm_w"], v["L2_xattn_k_norm_w"]], axis=1),
        "gate_w": tiled(v["L1_ffn_gate_w"]),
        "w_experts": experts,
        "w2": v["L2_ffn_w2"].reshape(P, 43, GROUP),
        "s2": v["L2_ffn_s2"].reshape(P, 43, 2),
        "w13": np.concatenate(packed, axis=2),
        "s13": np.concatenate(scales, axis=2),
        "w_cross": np.stack([tiled(v[f"L3_xattn_W{x}"].T).reshape(P, -1) for x in "qk"]),
        "b_cross": np.stack([v[f"L3_xattn_b{x}"].reshape(KT, P).T for x in "qk"], axis=1),
        "router_w": tiled(v["L3_ffn_router_weight"].T),
        "router_b": np.broadcast_to(v["L3_ffn_router_bias"], (P, ROUTED)),
        "expert_b": v["L3_ffn_expert_bias"],
    }
    arrays = {k: np.ascontiguousarray(a) for k, a in arrays.items()}
    nc = _bacc.Bacc("TRN2", target_bir_lowering=False, num_devices=1)
    ins = {k: nc.dram_tensor("in_" + k, a.shape, _mybir.dt.from_np(a.dtype), kind="ExternalInput").ap()
           for k, a in arrays.items()}
    out = nc.dram_tensor("out", (B, SQ, D), F32, kind="ExternalOutput").ap()
    build_program(nc, ins, out)
    r = _run(nc, [{"in_" + k: a for k, a in arrays.items()}], core_ids=[0])
    return r.results[0]["out"]
```
